# Optimizing a Trainium2 kernel written in Bass

```python
import numpy as np
import jax
import jax.numpy as jnp

def _softmax(x, axis=-1):
    return jax.nn.softmax(x, axis=axis)

def _gelu(x):
    return jax.nn.gelu(x, approximate=True)

def _silu(x):
    return jax.nn.silu(x)

def _sigmoid(x):
    return jax.nn.sigmoid(x)

def _layernorm(x, axis=-1, eps=1e-05):
    m = jnp.mean(x, axis=axis, keepdims=True)
    v = jnp.var(x, axis=axis, keepdims=True)
    return (x - m) / jnp.sqrt(v + eps)

def _scatter_add(tgt, idx, src, axis=0):
    return tgt.at[idx].add(src)

def _segment_sum(src, seg, n):
    return jax.ops.segment_sum(src, seg, n)
kernel_name = 'mk_decoder_postln_d1_seqx_r8_b52e7f'

def setup_inputs(seed: int=0):
    np.random.seed(seed)
    _w = jnp.asarray

    def _rec_inputs():
        import jax
        import jax.numpy as jnp
        _rk = jax.random.key(seed)
        x = 7.22e-05 + 1 * jax.random.normal(jax.random.fold_in(_rk, 1), (8, 256, 128), jnp.float32)
        _lenS = 256 - jax.random.randint(jax.random.fold_in(_rk, 7), (8,), 0, max(1, 256 // 4) + 1, jnp.int32)
        _lenS2 = 256 - jax.random.randint(jax.random.fold_in(_rk, 8), (8,), 0, max(1, 256 // 4) + 1, jnp.int32)
        _ctx_1024P = jax.random.normal(jax.random.fold_in(_rk, 11), (8, 16, 128), jnp.float32)
        _ctx_1024c = jax.random.dirichlet(jax.random.fold_in(_rk, 511), 0.3 * jnp.ones((16,), jnp.float32), (8, 256))
        _ctx_1024t = jnp.einsum('bsk,bkd->bsd', _ctx_1024c, _ctx_1024P)
        _ctx_1024t = _ctx_1024t * jax.lax.rsqrt(jnp.mean(jnp.square(_ctx_1024t)) + 1e-12) * 0.953939
        ctx_1024 = 4.13588e-05 + 0.999923 * (_ctx_1024t + 0.3 * jax.random.normal(jax.random.fold_in(_rk, 611), (8, 256, 128), jnp.float32))
        return (x, ctx_1024)
    x, ctx_1024 = _rec_inputs()

    def _L0_attn_setup():
        import jax, jax.numpy as jnp
        import numpy as np
        EMBED_DIM = 128
        NUM_HEADS = 16
        HEAD_DIM = EMBED_DIM // NUM_HEADS

        def _split_heads(t, B, T):
            return t.reshape(B, T, NUM_HEADS, HEAD_DIM).transpose(0, 2, 1, 3)
        key = jax.random.key(seed)
        ks = jax.random.split(key, 9)
        B, T, D = (2, 256, EMBED_DIM)
        s = 1.0 / np.sqrt(D)
        inp = {'x': jax.random.normal(ks[0], (B, T, D), dtype=jnp.float32), 'Wq': jax.random.normal(ks[1], (D, D), dtype=jnp.float32) * s, 'bq': jnp.zeros((D,), dtype=jnp.float32), 'Wk': jax.random.normal(ks[2], (D, D), dtype=jnp.float32) * s, 'bk': jnp.zeros((D,), dtype=jnp.float32), 'Wv': jax.random.normal(ks[3], (D, D), dtype=jnp.float32) * s, 'bv': jnp.zeros((D,), dtype=jnp.float32), 'Wo': jax.random.normal(ks[4], (D, D), dtype=jnp.float32) * s, 'bo': jnp.zeros((D,), dtype=jnp.float32)}
        return inp
    _L0_attn_all = _L0_attn_setup()
    _L0_attn_in = {k: v for k, v in _L0_attn_all.items() if k in ('Wq', 'bq', 'Wk', 'bk', 'Wv', 'bv', 'Wo', 'bo')}
    del _L0_attn_all

    def _L0_xattn_setup():
        import jax, jax.numpy as jnp
        import numpy as np
        D_MODEL = 128
        HEADS = 16
        D_K = D_MODEL // HEADS
        key = jax.random.key(seed)
        ks = jax.random.split(key, 11)
        B, S = (4, 256)
        s = 1.0 / np.sqrt(D_MODEL)
        return {'q': jax.random.normal(ks[0], (B, S, D_MODEL), dtype=jnp.float32), 'k': jax.random.normal(ks[1], (B, S, D_MODEL), dtype=jnp.float32), 'v': jax.random.normal(ks[2], (B, S, D_MODEL), dtype=jnp.float32), 'Wq': jax.random.normal(ks[3], (D_MODEL, D_MODEL), dtype=jnp.float32) * s, 'bq': jnp.zeros((D_MODEL,), dtype=jnp.float32), 'Wk': jax.random.normal(ks[4], (D_MODEL, D_MODEL), dtype=jnp.float32) * s, 'bk': jnp.zeros((D_MODEL,), dtype=jnp.float32), 'Wv': jax.random.normal(ks[5], (D_MODEL, D_MODEL), dtype=jnp.float32) * s, 'bv': jnp.zeros((D_MODEL,), dtype=jnp.float32), 'Wo': jax.random.normal(ks[6], (D_MODEL, D_MODEL), dtype=jnp.float32) * s, 'bo': jnp.zeros((D_MODEL,), dtype=jnp.float32)}
    _L0_xattn_all = _L0_xattn_setup()
    _L0_xattn_in = {k: v for k, v in _L0_xattn_all.items() if k in ('Wq', 'bq', 'Wk', 'bk', 'Wv', 'bv', 'Wo', 'bo')}
    del _L0_xattn_all

    def _L0_ffn_setup():
        import jax, jax.numpy as jnp
        import numpy as np
        DIM = 128
        DEPTH = 2
        HEADS = 8
        DIM_HEAD = 64
        WINDOW = 64
        INNER = HEADS * DIM_HEAD
        HID = int(DIM * 4 * 2 / 3)
        B, N = (2, 1024)
        QK_SCALE = 8.0

        def shift_token(t):
            t1, t2 = jnp.split(t, 2, axis=-1)
            t2 = jnp.pad(t2, ((0, 0), (1, 0), (0, 0)))[:, :-1]
            return jnp.concatenate([t1, t2], axis=-1)

        def l2norm(t):
            return t / jnp.clip(jnp.linalg.norm(t, axis=-1, keepdims=True), 1e-12)

        def rotate_half(x):
            x1, x2 = jnp.split(x, 2, axis=-1)
            return jnp.concatenate([-x2, x1], axis=-1)

        def rotary_xpos(q, k):
            n = q.shape[-2]
            half_idx = jnp.arange(0, DIM_HEAD, 2, dtype=jnp.float32)
            inv_freq = 1.0 / 10000.0 ** (half_idx / DIM_HEAD)
            t = jnp.arange(n, dtype=jnp.float32)
            freqs = t[:, None] * inv_freq[None, :]
            freqs = jnp.concatenate([freqs, freqs], axis=-1)
            base = (half_idx + 0.4 * DIM_HEAD) / (1.4 * DIM_HEAD)
            power = (t - n // 2) / float(WINDOW // 2)
            scale = base[None, :] ** power[:, None]
            scale = jnp.concatenate([scale, scale], axis=-1)
            cos, sin = (jnp.cos(freqs), jnp.sin(freqs))
            q = q * cos * scale + rotate_half(q) * sin * scale
            k = k * cos / scale + rotate_half(k) * sin / scale
            return (q, k)

        def local_attention(q, k, v):
            b, h, n, d = q.shape
            w = n // WINDOW
            bq = q.reshape(b, h, w, WINDOW, d) * QK_SCALE
            bk = k.reshape(b, h, w, WINDOW, d)
            bv = v.reshape(b, h, w, WINDOW, d)

            def look_around(t):
                p = jnp.pad(t, ((0, 0), (0, 0), (1, 0), (0, 0), (0, 0)))
                return jnp.concatenate([p[:, :, :w], p[:, :, 1:]], axis=3)
            bk, bv = (look_around(bk), look_around(bv))
            bt = jnp.arange(n).reshape(w, WINDOW)
            btp = jnp.pad(bt, ((1, 0), (0, 0)), constant_values=-1)
            btk = jnp.concatenate([btp[:w], btp[1:]], axis=1)
            sim = jnp.einsum('bhwid,bhwjd->bhwij', bq, bk)
            i = bt[:, :, None]
            j = btk[:, None, :]
            mask = (i < j) | (i > j + WINDOW) | (j == -1)
            sim = jnp.where(mask, -jnp.finfo(sim.dtype).max, sim)
            attn = jax.nn.softmax(sim, axis=-1)
            out = jnp.einsum('bhwij,bhwjd->bhwid', attn, bv)
            return out.reshape(b, h, n, d)

        def _layer(x, wqkv, qs, ksc, wo, lg, lb, w1, b1, w2, b2):
            b, n, _ = x.shape
            h = shift_token(x)
            qkv = h @ wqkv
            q, k, v = jnp.split(qkv, 3, axis=-1)
            to_heads = lambda t: t.reshape(b, n, HEADS, DIM_HEAD).transpose(0, 2, 1, 3)
            q, k, v = (to_heads(q), to_heads(k), to_heads(v))
            q = l2norm(q) * qs
            k = l2norm(k) * ksc
            q, k = rotary_xpos(q, k)
            o = local_attention(q, k, v)
            o = o.transpose(0, 2, 1, 3).reshape(b, n, INNER)
            x = x + o @ wo
            h = shift_token(x)
            mu = h.mean(-1, keepdims=True)
            var = h.var(-1, keepdims=True)
            h = (h - mu) / jnp.sqrt(var + 1e-05) * lg + lb
            h = h @ w1 + b1
            a, g = jnp.split(h, 2, axis=-1)
            h = a * jax.nn.gelu(g, approximate=False)
            x = x + h @ w2 + b2
            return x
        key = jax.random.key(seed)
        ks = jax.random.split(key, 6)
        return {'x': jax.random.normal(ks[0], (B, N, DIM), jnp.float32), 'wqkv': jax.random.normal(ks[1], (DEPTH, DIM, 3 * INNER), jnp.float32) * 0.02, 'q_scale': jnp.ones((DEPTH, DIM_HEAD), jnp.float32), 'k_scale': jnp.ones((DEPTH, DIM_HEAD), jnp.float32), 'wo': jax.random.normal(ks[2], (DEPTH, INNER, DIM), jnp.float32) * 0.02, 'ln_g': jnp.ones((DEPTH, DIM), jnp.float32), 'ln_b': jnp.zeros((DEPTH, DIM), jnp.float32), 'w1': jax.random.normal(ks[3], (DEPTH, DIM, 2 * HID), jnp.float32) * 0.02, 'b1': jnp.zeros((DEPTH, 2 * HID), jnp.float32), 'w2': jax.random.normal(ks[4], (DEPTH, HID, DIM), jnp.float32) * 0.02, 'b2': jnp.zeros((DEPTH, DIM), jnp.float32)}
    _L0_ffn_all = _L0_ffn_setup()
    _L0_ffn_in = {k: v for k, v in _L0_ffn_all.items() if k in ('wqkv', 'q_scale', 'k_scale', 'wo', 'ln_g', 'ln_b', 'w1', 'b1', 'w2', 'b2')}
    del _L0_ffn_all
    return {'x': x, 'ctx_1024': ctx_1024, 'L0_attn_Wq': _L0_attn_in['Wq'], 'L0_attn_bq': _L0_attn_in['bq'], 'L0_attn_Wk': _L0_attn_in['Wk'], 'L0_attn_bk': _L0_attn_in['bk'], 'L0_attn_Wv': _L0_attn_in['Wv'], 'L0_attn_bv': _L0_attn_in['bv'], 'L0_attn_Wo': _L0_attn_in['Wo'], 'L0_attn_bo': _L0_attn_in['bo'], 'L0_xattn_Wq': _L0_xattn_in['Wq'], 'L0_xattn_bq': _L0_xattn_in['bq'], 'L0_xattn_Wk': _L0_xattn_in['Wk'], 'L0_xattn_bk': _L0_xattn_in['bk'], 'L0_xattn_Wv': _L0_xattn_in['Wv'], 'L0_xattn_bv': _L0_xattn_in['bv'], 'L0_xattn_Wo': _L0_xattn_in['Wo'], 'L0_xattn_bo': _L0_xattn_in['bo'], 'L0_ffn_wqkv': _L0_ffn_in['wqkv'], 'L0_ffn_q_scale': _L0_ffn_in['q_scale'], 'L0_ffn_k_scale': _L0_ffn_in['k_scale'], 'L0_ffn_wo': _L0_ffn_in['wo'], 'L0_ffn_ln_g': _L0_ffn_in['ln_g'], 'L0_ffn_ln_b': _L0_ffn_in['ln_b'], 'L0_ffn_w1': _L0_ffn_in['w1'], 'L0_ffn_b1': _L0_ffn_in['b1'], 'L0_ffn_w2': _L0_ffn_in['w2'], 'L0_ffn_b2': _L0_ffn_in['b2']}

def reference(x, ctx_1024, L0_attn_Wq, L0_attn_bq, L0_attn_Wk, L0_attn_bk, L0_attn_Wv, L0_attn_bv, L0_attn_Wo, L0_attn_bo, L0_xattn_Wq, L0_xattn_bq, L0_xattn_Wk, L0_xattn_bk, L0_xattn_Wv, L0_xattn_bv, L0_xattn_Wo, L0_xattn_bo, L0_ffn_wqkv, L0_ffn_q_scale, L0_ffn_k_scale, L0_ffn_wo, L0_ffn_ln_g, L0_ffn_ln_b, L0_ffn_w1, L0_ffn_b1, L0_ffn_w2, L0_ffn_b2):
    import jax
    import jax.numpy as jnp

    def _L0_attn_ref(x, Wq, bq, Wk, bk, Wv, bv, Wo, bo):
        import jax, jax.numpy as jnp
        import numpy as np
        EMBED_DIM = 128
        NUM_HEADS = 16
        HEAD_DIM = EMBED_DIM // NUM_HEADS

        def _split_heads(t, B, T):
            return t.reshape(B, T, NUM_HEADS, HEAD_DIM).transpose(0, 2, 1, 3)
        B, T, D = x.shape
        q = _split_heads(x @ Wq.T + bq, B, T)
        k = _split_heads(x @ Wk.T + bk, B, T)
        v = _split_heads(x @ Wv.T + bv, B, T)
        scaling = 1.0 / np.sqrt(HEAD_DIM).astype(np.float32)
        scores = jnp.einsum('bhqd,bhkd->bhqk', q, k) * scaling
        causal = jnp.tril(jnp.ones((T, T), dtype=bool))
        scores = jnp.where(causal, scores, -jnp.inf)
        attn = jax.nn.softmax(scores, axis=-1)
        ctx = jnp.einsum('bhqk,bhkd->bhqd', attn, v)
        ctx = ctx.transpose(0, 2, 1, 3).reshape(B, T, D)
        return ctx @ Wo.T + bo

    def _L0_xattn_ref(q, k, v, Wq, bq, Wk, bk, Wv, bv, Wo, bo):
        import jax, jax.numpy as jnp
        import numpy as np
        D_MODEL = 128
        HEADS = 16
        D_K = D_MODEL // HEADS
        B, S, _ = q.shape

        def proj(x, W, b):
            return (x @ W.T + b).reshape(B, -1, HEADS, D_K).transpose(0, 2, 1, 3)
        qh = proj(q, Wq, bq)
        kh = proj(k, Wk, bk)
        vh = proj(v, Wv, bv)
        scores = jnp.einsum('bhqd,bhkd->bhqk', qh, kh) / jnp.sqrt(jnp.float32(D_K))
        attn = jax.nn.softmax(scores, axis=-1)
        out = jnp.einsum('bhqk,bhkd->bhqd', attn, vh)
        concat = out.transpose(0, 2, 1, 3).reshape(B, S, D_MODEL)
        return concat @ Wo.T + bo

    def _L0_ffn_ref(x, wqkv, q_scale, k_scale, wo, ln_g, ln_b, w1, b1, w2, b2):
        import jax, jax.numpy as jnp
        import numpy as np
        DIM = 128
        DEPTH = 2
        HEADS = 8
        DIM_HEAD = 64
        WINDOW = 64
        INNER = HEADS * DIM_HEAD
        HID = int(DIM * 4 * 2 / 3)
        B, N = (2, 1024)
        QK_SCALE = 8.0

        def shift_token(t):
            t1, t2 = jnp.split(t, 2, axis=-1)
            t2 = jnp.pad(t2, ((0, 0), (1, 0), (0, 0)))[:, :-1]
            return jnp.concatenate([t1, t2], axis=-1)

        def l2norm(t):
            return t / jnp.clip(jnp.linalg.norm(t, axis=-1, keepdims=True), 1e-12)

        def rotate_half(x):
            x1, x2 = jnp.split(x, 2, axis=-1)
            return jnp.concatenate([-x2, x1], axis=-1)

        def rotary_xpos(q, k):
            n = q.shape[-2]
            half_idx = jnp.arange(0, DIM_HEAD, 2, dtype=jnp.float32)
            inv_freq = 1.0 / 10000.0 ** (half_idx / DIM_HEAD)
            t = jnp.arange(n, dtype=jnp.float32)
            freqs = t[:, None] * inv_freq[None, :]
            freqs = jnp.concatenate([freqs, freqs], axis=-1)
            base = (half_idx + 0.4 * DIM_HEAD) / (1.4 * DIM_HEAD)
            power = (t - n // 2) / float(WINDOW // 2)
            scale = base[None, :] ** power[:, None]
            scale = jnp.concatenate([scale, scale], axis=-1)
            cos, sin = (jnp.cos(freqs), jnp.sin(freqs))
            q = q * cos * scale + rotate_half(q) * sin * scale
            k = k * cos / scale + rotate_half(k) * sin / scale
            return (q, k)

        def local_attention(q, k, v):
            b, h, n, d = q.shape
            w = n // WINDOW
            bq = q.reshape(b, h, w, WINDOW, d) * QK_SCALE
            bk = k.reshape(b, h, w, WINDOW, d)
            bv = v.reshape(b, h, w, WINDOW, d)

            def look_around(t):
                p = jnp.pad(t, ((0, 0), (0, 0), (1, 0), (0, 0), (0, 0)))
                return jnp.concatenate([p[:, :, :w], p[:, :, 1:]], axis=3)
            bk, bv = (look_around(bk), look_around(bv))
            bt = jnp.arange(n).reshape(w, WINDOW)
            btp = jnp.pad(bt, ((1, 0), (0, 0)), constant_values=-1)
            btk = jnp.concatenate([btp[:w], btp[1:]], axis=1)
            sim = jnp.einsum('bhwid,bhwjd->bhwij', bq, bk)
            i = bt[:, :, None]
            j = btk[:, None, :]
            mask = (i < j) | (i > j + WINDOW) | (j == -1)
            sim = jnp.where(mask, -jnp.finfo(sim.dtype).max, sim)
            attn = jax.nn.softmax(sim, axis=-1)
            out = jnp.einsum('bhwij,bhwjd->bhwid', attn, bv)
            return out.reshape(b, h, n, d)

        def _layer(x, wqkv, qs, ksc, wo, lg, lb, w1, b1, w2, b2):
            b, n, _ = x.shape
            h = shift_token(x)
            qkv = h @ wqkv
            q, k, v = jnp.split(qkv, 3, axis=-1)
            to_heads = lambda t: t.reshape(b, n, HEADS, DIM_HEAD).transpose(0, 2, 1, 3)
            q, k, v = (to_heads(q), to_heads(k), to_heads(v))
            q = l2norm(q) * qs
            k = l2norm(k) * ksc
            q, k = rotary_xpos(q, k)
            o = local_attention(q, k, v)
            o = o.transpose(0, 2, 1, 3).reshape(b, n, INNER)
            x = x + o @ wo
            h = shift_token(x)
            mu = h.mean(-1, keepdims=True)
            var = h.var(-1, keepdims=True)
            h = (h - mu) / jnp.sqrt(var + 1e-05) * lg + lb
            h = h @ w1 + b1
            a, g = jnp.split(h, 2, axis=-1)
            h = a * jax.nn.gelu(g, approximate=False)
            x = x + h @ w2 + b2
            return x
        for l in range(DEPTH):
            x = _layer(x, wqkv[l], q_scale[l], k_scale[l], wo[l], ln_g[l], ln_b[l], w1[l], b1[l], w2[l], b2[l])
        return x
    x = _layernorm(x + _L0_attn_ref(x, L0_attn_Wq, L0_attn_bq, L0_attn_Wk, L0_attn_bk, L0_attn_Wv, L0_attn_bv, L0_attn_Wo, L0_attn_bo), axis=-1)
    x = _layernorm(x + _L0_xattn_ref(x, ctx_1024, ctx_1024, L0_xattn_Wq, L0_xattn_bq, L0_xattn_Wk, L0_xattn_bk, L0_xattn_Wv, L0_xattn_bv, L0_xattn_Wo, L0_xattn_bo), axis=-1)
    x = _layernorm(x + _L0_ffn_ref(x, L0_ffn_wqkv, L0_ffn_q_scale, L0_ffn_k_scale, L0_ffn_wo, L0_ffn_ln_g, L0_ffn_ln_b, L0_ffn_w1, L0_ffn_b1, L0_ffn_w2, L0_ffn_b2), axis=-1)
    return x

_drawn_inputs = setup_inputs


def setup_inputs(seed=0):
    import zlib

    import numpy as np

    out = dict(_drawn_inputs(seed))
    spreads = {'L0_attn_bq': (0.0, 0.511),
     'L0_attn_bk': (0.0, 2.0),
     'L0_attn_bv': (0.0, 0.1),
     'L0_attn_bo': (0.0, 0.1),
     'L0_xattn_bq': (0.0, 0.393),
     'L0_xattn_bk': (0.0, 2.0),
     'L0_xattn_bv': (0.0, 0.1),
     'L0_xattn_bo': (0.0, 0.1),
     'L0_ffn_q_scale': (1.0, 0.6),
     'L0_ffn_k_scale': (1.0, 0.6),
     'L0_ffn_ln_g': (1.0, 0.6),
     'L0_ffn_ln_b': (0.0, 0.8),
     'L0_ffn_b1': (0.0, 0.8),
     'L0_ffn_b2': (0.0, 0.556)}
    factors = {'L0_ffn_w1': 6.215, 'L0_ffn_w2': 6.108}
    for name, (base, spread) in spreads.items():
        noise = np.random.default_rng([zlib.crc32(name.encode()), seed]).standard_normal(out[name].shape)
        drawn = base * np.exp(spread * noise) if base else spread * noise
        out[name] = jnp.asarray(drawn.astype(out[name].dtype))
    for name, factor in factors.items():
        out[name] = (out[name] * factor).astype(out[name].dtype)
    return out
```

```python
from contextlib import ExitStack

import concourse.bass as bass
from concourse import mybir

F32 = mybir.dt.float32
F32R = mybir.dt.float32r
BF16 = mybir.dt.bfloat16
ALU = mybir.AluOpType
ACT = mybir.ActivationFunctionType
AX = mybir.AxisListType

P = 128
B = 8
T = 256
NT = T // P
H = 16
HD = 8
G = H // 4
EPS = 1e-5
STAGES = ("self", "cross", "ffn")
SM_SCALE = float(1.0 / (HD ** 0.5))


def ds(start, size):
    return bass.ds(start, size)


class Shared:
    pass


def apart(eng, sh):
    eng.sem_inc(sh.passed, 1)


class AttnMisc:

    FULL = ["xT", "v", "oT1", "mT1", "cT", "wo", "oT0", "mT0"]
    FIRST = {-1: ["xT", "v", "mT0"], 0: ["xT", "v", "mT1", "oT0", "mT0"],
             B - 1: ["oT1", "mT1", "cT", "wo", "oT0"], B: ["oT1", "cT", "wo"]}

    @classmethod
    def before(cls, step, use):
        if isinstance(step, int) and step in cls.FIRST:
            base = {-1: 0, 0: 3, B - 1: 8 * (B - 1), B: 8 * (B - 1) + 5}[step]
            return base + cls.FIRST[step].index(use)
        return step * 8 + cls.FULL.index(use)


def attention_stage(nc, sh, name, causal, dram, x_dram, ctx_dram):
    Wq, Wk, Wv, Wo, bq, bk, bv, bo = dram
    cross = ctx_dram is not None
    ctx = ExitStack()
    with ctx:
        def sb(what, shape, dt=F32):
            return ctx.enter_context(nc.sbuf_tensor(f"{name}_{what}", shape, dt))

        def sem(what):
            return sh.stack.enter_context(nc.semaphore(f"{name}_{what}"))

        w_raw = sb("w_raw", [P, 4, P])
        wT = sb("wT", [P, 4, P])
        wS = sb("wS", [P, 2, G, 4, 32])
        brow = sb("brow", [1, 2, H, HD])
        bS = sb("bS", [1, 2, G, 4, 32])
        selrow = sb("selrow", [1, 2, 4, 32])
        cols = sb("cols", [P, 2, G + 1])
        cols_s = sb("cols_s", [P, 2, G])
        bvB = sb("bvB", [P, P])
        boB = sb("boB", [P, P])

        x_in = sb("x_in", [P, 2, NT, P])
        c_in = sb("c_in", [P, 2, NT, P]) if cross else x_in
        xT = sb("xT", [P, 2, T])
        cT = sb("cT", [P, 2, T]) if cross else xT
        x_res = sb("x_res", [P, 2, NT, P])
        low = sb("low", [P, 2, T])
        qs = sb("qs", [P, 2, G, T], F32R)
        ks = sb("ks", [P, 2, G, T], F32R)
        qm = sb("qm", [P, 2, G, T], F32R)
        va = sb("va", [P, 2, NT, H, 32])
        probs = sb("probs", [P, 4, 2, 2, T])
        negmax = sb("negmax", [P, 2, NT, H])
        msp = sb("msp", [P, 2, NT, H, 32])
        o_sb = sb("o_sb", [P, 2, 2, T])
        rden = sb("rden", [P, 2, NT, 2, 4])
        ctxn = sb("ctxn", [P, NT, P])
        ctxT = sb("ctxT", [P, T])
        y = sb("y", [P, NT, P])
        stats = sb("stats", [P, NT, 6])
        mv = sb("mv", [P, NT, 2])
        lnv = sb("lnv", [P, NT])
        rstd = sb("rstd", [P, NT])

        bank = sh.bank
        S, TB, O, PR, MISC = bank[0:2], bank[2:4], bank[4:6], bank[6], bank[7]

        loaded = sem("loaded")
        prep_pe = sem("prep_pe")
        prep_dve = sem("prep_dve")
        prep_pool = sem("prep_pool")
        cleared = sem("cleared")
        x_loaded = [sem("x_loaded0"), sem("x_loaded1")]
        c_loaded = [sem("c_loaded0"), sem("c_loaded1")] if cross else x_loaded
        x_copied = sem("x_copied")
        res_ready = sem("res_ready")
        misc_done = sem("misc_done")
        misc_free = sem("misc_free")
        proj_done = sem("proj_done")
        low_ready = sem("low_ready")
        proj_out = sem("proj_out")
        s_done = sem("s_done")
        max_done = sem("max_done")
        mhi_ready = sem("mhi_ready")
        msp_ready = sem("msp_ready")
        st_done = sem("st_done")
        exp_done = sem("exp_done")
        pv_done = sem("pv_done")
        o_out = sem("o_out")
        rden_ready = sem("rden_ready")
        ctx_ready = sem("ctx_ready")
        stats_ready = sem("stats_ready")
        mv_ready = sem("mv_ready")
        ln_ready = sem("ln_ready")
        rstd_ready = sem("rstd_ready")
        x_ready = sem("x_ready")

        PARTS = (0, 1, 4, 5)
        before = AttnMisc.before

        def wait(eng, s, value):
            if not isinstance(value, int) or value > 0:
                eng.wait_ge(s, value)

        def misc_begin(eng, step, use):
            wait(eng, misc_free, before(step, use))

        def misc_filled(eng, step, use):
            eng.wait_ge(misc_done, before(step, use) + 1)

        def misc_read(eng, step, use):
            eng.wait_ge(misc_free, before(step, use) + 1)

        def steps(eng, body, last_step=True):
            body(-1, 0)
            body(0, 1)
            with eng.Fori(0, (B - 2) // 2) as i:
                body(i * 2 + 1, 0)
                body(i * 2 + 2, 1)
            body(B - 1, 0)
            body(B, 1)

        def has_front(step):
            return not isinstance(step, int) or step < B - 1

        def has_mid(step):
            return not isinstance(step, int) or 0 <= step < B

        def has_tail(step):
            return not isinstance(step, int) or step > 0

        block = ctx.enter_context(nc.Block())

        @block.sync
        def _(eng):
            for n, w in enumerate((Wq, Wk, Wv, Wo)):
                eng.dma_start(w_raw[:, n, :], w).then_inc(loaded, 16)
            eng.dma_start(brow[0:1, 0, :, :], bq.rearrange("(a h d) -> a h d", a=1, d=HD)).then_inc(loaded, 16)
            eng.dma_start(brow[0:1, 1, :, :], bk.rearrange("(a h d) -> a h d", a=1, d=HD)).then_inc(loaded, 16)
            eng.dma_start(bvB[:, :], bv.partition_broadcast(P)).then_inc(loaded, 16)
            eng.dma_start(boB[:, :], bo.partition_broadcast(P)).then_inc(loaded, 16)

            def load(n, ring):
                if not (isinstance(n, int) and n < 2):
                    misc_read(eng, n - 3, "xT")
                    apart(eng, sh)
                    eng.wait_ge(res_ready, n - 1)
                    apart(eng, sh)
                if not cross:
                    eng.dma_start(x_in[:, ring, :, :], x_dram[:, ds(n * NT, NT), :]).then_inc(x_loaded[ring], 16)
                else:
                    eng.dma_start(c_in[:, ring, :, :], ctx_dram[:, ds(n * NT, NT), :]).then_inc(c_loaded[ring], 16)

            load(0, 0)
            load(1, 1)
            load(2, 0)
            load(3, 1)
            with eng.Fori(0, (B - 4) // 2) as i:
                load(i * 2 + 4, 0)
                load(i * 2 + 5, 1)

        @block.gpsimd
        def _(eng):
            eng.memset(va[:], 0.0).then_inc(prep_pool, 1)
            eng.wait_ge(prep_pool, 1)
            eng.memset(va[:, :, :, :, HD:HD + 1], 1.0).then_inc(prep_pool, 1)
            eng.memset(msp[:], 0.0).then_inc(prep_pool, 1)
            eng.wait_ge(loaded, 128)

            def batch(n, ring):
                if cross:
                    if not (isinstance(n, int) and n < 2):
                        misc_read(eng, n - 3, "xT")
                    apart(eng, sh)
                    eng.tensor_copy(x_in[:, ring, :, :], sh.x[:, ds(n * NT, NT), :]).then_inc(x_copied, 1)
                    eng.wait_ge(x_copied, n + 1)
                else:
                    half = n // 2 if isinstance(n, int) else (n - ring) // 2
                    eng.wait_ge(x_loaded[ring], half * 16 + 16)
                if not (isinstance(n, int) and n < 2):
                    misc_read(eng, n - 1, "wo")
                for t in range(NT):
                    add = eng.tensor_tensor(x_res[:, ring, t, :], x_in[:, ring, t, :], boB[:, :], ALU.add)
                add.then_inc(res_ready, 1)

            for n in range(4):
                batch(n, n % 2)
            with eng.Fori(0, (B - 4) // 2) as i:
                batch(i * 2 + 4, 0)
                batch(i * 2 + 5, 1)

        @block.tensor
        def _(eng):
            eng.wait_ge(loaded, 128)
            for n in range(4):
                tr = eng.transpose(MISC[:, n * P:n * P + P], w_raw[:, n, :], sh.ident[:, :])
            tr.then_inc(prep_pe, 1)
            eng.wait_ge(prep_dve, 1)
            for n in range(2):
                for g in range(G):
                    eng.matmul(PR[:, n * 8 + g:n * 8 + g + 1],
                               bS[0:1, n, g, :, :].rearrange("p j c -> p (j c)"), sh.one[0:1, 0:1],
                               start=True, stop=True)
                mm = eng.matmul(PR[:, n * 8 + G:n * 8 + G + 1],
                                selrow[0:1, n, :, :].rearrange("p j c -> p (j c)"), sh.one[0:1, 0:1],
                                start=True, stop=True)
            mm.then_inc(prep_pe, 1)
            eng.wait_ge(prep_dve, 2)
            eng.wait_ge(prep_pool, 3)

            def in_transposes(n, ring):
                misc_begin(eng, n - 1, "xT")
                if cross:
                    eng.wait_ge(x_copied, n + 1)
                half = n // 2 if isinstance(n, int) else (n - ring) // 2
                eng.wait_ge(c_loaded[ring], half * 16 + 16)
                for t in range(NT):
                    tr = eng.transpose(MISC[:, t * P:t * P + P], x_in[:, ring, t, :], sh.ident[:, :])
                if cross:
                    for t in range(NT):
                        tr = eng.transpose(MISC[:, T + t * P:T + t * P + P], c_in[:, ring, t, :], sh.ident[:, :])
                tr.then_inc(misc_done, 1)

            def project(n, ring, k):
                gp, which = k // 2, k % 2
                if k == 0:
                    misc_read(eng, n - 1, "xT")
                wait(eng, proj_out, n * 4 + k)
                src = xT if which == 0 else cT
                for gi in range(2):
                    mm = eng.matmul(PR[:, gi * T:gi * T + T],
                                    wS[:, which, 2 * gp + gi, :, :].rearrange("p j c -> p (j c)"),
                                    src[:, ring, :], start=True, stop=True)
                mm.then_inc(proj_done, 1)


            def scores(n, ring, u):
                gp, jp, t = u // 4, u % 4 // 2, u % 2
                if u % 4 == 0:
                    eng.wait_ge(proj_out, n * 4 + 2 * gp + 2)
                wait(eng, max_done, n * 8 + u)
                for gi in range(2):
                    for jj in range(2):
                        p = 32 * (2 * jp + jj)
                        mm = eng.matmul(S[jj][:, gi * T:gi * T + T],
                                        qs[p:p + 32, ring, 2 * gp + gi, t * P:t * P + P],
                                        ks[p:p + 32, ring, 2 * gp + gi, :], start=True, stop=not causal)
                    if causal:
                        for bank in S:
                            mm = eng.matmul(bank[:, gi * T + t * P:gi * T + t * P + P], sh.ident_b[:, :],
                                            sh.causal[:, :], start=False, stop=True)
                mm.then_inc(s_done, 1)

            def scores_T(n, ring, u):
                gp, jp, t = u // 4, u % 4 // 2, u % 2
                if u % 4 == 0:
                    misc_read(eng, n if u else n - 1, "mT1" if u else "mT0")
                wait(eng, exp_done, n * 8 + u)
                for gi in range(2):
                    for jj in range(2):
                        p = 32 * (2 * jp + jj)
                        mm = eng.matmul(TB[jj][:, gi * T:gi * T + T],
                                        ks[p:p + 32, ring, 2 * gp + gi, t * P:t * P + P],
                                        qm[p:p + 32, ring, 2 * gp + gi, :], start=True, stop=not causal)
                    if causal:
                        for bank in TB:
                            mm = eng.matmul(bank[:, gi * T + t * P:gi * T + t * P + P], sh.ident_b[:, :],
                                            sh.causal_T[:, :], start=False, stop=True)
                mm.then_inc(st_done, 1)

            def values(n, ring, w):
                gp, jp, gi = w // 4, w % 4 // 2, w % 2
                eng.wait_ge(exp_done, n * 8 + 2 * (w // 2) + 2)
                if w == 0:
                    misc_read(eng, n - 1, "v")
                if w % 4 == 0:
                    wait(eng, o_out, n * 2 + gp - 1)
                for t in range(NT):
                    q0 = t * P if causal else 0
                    for jj in range(2):
                        j = 2 * jp + jj
                        mm = eng.matmul(O[gp][32 * j:32 * j + 32, gi * T + q0:gi * T + T],
                                        va[:, ring, t, 4 * (2 * gp + gi) + j, :],
                                        probs[:, (2 * (w // 2) + t) % 4, jj, gi, q0:T],
                                        start=(t == 0), stop=(t == NT - 1))
                mm.then_inc(pv_done, 1)

            def max_transposes(step, n, ring, gp):
                use = f"mT{gp}"
                misc_begin(eng, step, use)
                eng.wait_ge(msp_ready, n * 2 + gp + 1)
                for gi in range(2):
                    for t in range(NT):
                        g = 2 * gp + gi
                        tr = eng.transpose(MISC[:, gi * T + t * P:gi * T + t * P + P],
                                           msp[:, ring, t, 4 * g:4 * g + 4, :].rearrange("p h c -> p (h c)"),
                                           sh.ident[:, :])
                tr.then_inc(misc_done, 1)

            def out_transposes(step, n, gp):
                misc_begin(eng, step, f"oT{gp}")
                eng.wait_ge(o_out, n * 2 + gp + 1)
                for t in range(NT):
                    for gi in range(2):
                        tr = eng.transpose(MISC[:, (t * 2 + gi) * P:(t * 2 + gi) * P + P],
                                           o_sb[:, gp, gi, t * P:t * P + P], sh.ident[:, :])
                tr.then_inc(misc_done, 1)

            def step(b, other):
                own = 1 - other
                for slot in range(8):
                    if has_front(b) and slot == 0:
                        in_transposes(b + 1, other)
                    if has_mid(b):
                        scores_T(b, own, slot)
                    if has_tail(b) and slot < 2:
                        values(b - 1, other, slot + 6)
                    if has_mid(b) and slot >= 2:
                        values(b, own, slot - 2)
                    if has_front(b) and slot in PARTS:
                        project(b + 1, other, PARTS.index(slot))
                    if has_front(b) and slot == 7:
                        max_transposes(b, b + 1, other, 0)
                    if has_mid(b) and slot == 3:
                        max_transposes(b, b, own, 1)
                    if has_mid(b) and slot < 2:
                        scores(b, own, slot + 6)
                    if has_front(b) and slot >= 2:
                        scores(b + 1, other, slot - 2)
                    if has_tail(b):
                        if slot == 2:
                            out_transposes(b, b - 1, 1)
                        if slot == 4:
                            misc_begin(eng, b, "cT")
                            eng.wait_ge(ctx_ready, (b - 1) * 4 + 4)
                            for t in range(NT):
                                tr = eng.transpose(MISC[:, t * P:t * P + P], ctxn[:, t, :], sh.ident[:, :])
                            tr.then_inc(misc_done, 1)
                        if slot == 5:
                            misc_begin(eng, b, "wo")
                            for t in range(NT):
                                mm = eng.matmul(MISC[:, t * P:t * P + P], ctxT[:, t * P:t * P + P],
                                                wT[:, 3, :], start=True, stop=True)
                            mm.then_inc(misc_done, 1)
                    if has_front(b) and slot == 1:
                        misc_begin(eng, b, "v")
                        for t in range(NT):
                            mm = eng.matmul(MISC[:, t * P:t * P + P], cT[:, other, t * P:t * P + P],
                                            wT[:, 2, :], start=True, stop=True)
                        mm.then_inc(misc_done, 1)
                    if has_mid(b) and slot == 6:
                        out_transposes(b, b, 0)

            steps(eng, step)

        @block.scalar
        def _(eng):
            eng.preload_act_table_set("natural_log_exp_and_others")
            eng.wait_ge(prep_dve, 3)

            def exps(n, u):
                wait(eng, pv_done, n * 8 + 2 * (u // 2) - 2)
                eng.wait_ge(st_done, n * 8 + u + 1)
                q0 = (u % 2) * P if causal else 0
                eng.activation(probs[:, u % 4, :, :, q0:T],
                               sh.banks[1][:, :].rearrange("p (b a q) -> p b a q", b=2, a=2)[:, :, :, q0:T],
                               ACT.Exp, scale=SM_SCALE).then_inc(exp_done, 1)

            def evac_out(n, gp):
                eng.wait_ge(pv_done, n * 8 + 4 * gp + 4)
                eng.activation(o_sb[:, gp, :, :].rearrange("p g q -> p (g q)"), O[gp][:, :],
                               ACT.Copy).then_inc(o_out, 1)

            def step(b, other):
                for slot in range(8):
                    if has_front(b) and slot == 0:
                        misc_filled(eng, b, "xT")
                        if cross:
                            eng.activation(cT[:, other, :], MISC[:, T:2 * T], ACT.Copy)
                        eng.activation(xT[:, other, :], MISC[:, 0:T], ACT.Copy).then_inc(misc_free, 1)
                    if has_mid(b):
                        exps(b, slot)
                    if has_tail(b) and slot == 1:
                        evac_out(b - 1, 1)
                    if has_mid(b) and slot == 5:
                        evac_out(b, 0)
                    if has_front(b) and slot in PARTS:
                        k = PARTS.index(slot)
                        gp, which = k // 2, k % 2
                        eng.wait_ge(proj_done, (b + 1) * 4 + k + 1)
                        for gi in range(2):
                            g = 2 * gp + gi
                            hi = eng.activation(low[:, gi, :].bitcast(F32R), PR[:, gi * T:gi * T + T],
                                                ACT.Identity, bias=cols_s[:, which, g:g + 1],
                                                scale=cols[:, which, G:G + 1])
                        hi.then_inc(low_ready, 1)
                    if has_tail(b):
                        if slot == 4:
                            misc_filled(eng, b, "cT")
                            eng.activation(ctxT[:, :], MISC[:, 0:T], ACT.Copy).then_inc(misc_free, 1)
                        if slot == 6:
                            eng.wait_ge(mv_ready, b)
                            eng.activation(lnv[:, :], mv[:, :, 1], ACT.Ln, bias=sh.eps[:, 0:1]).then_inc(ln_ready, 1)
                            eng.wait_ge(ln_ready, b)
                            eng.activation(rstd[:, :], lnv[:, :], ACT.Exp, scale=-0.5).then_inc(rstd_ready, 1)

            steps(eng, step)

        @block.vector
        def _(eng):
            eng.memset(bS[:], 0.0).then_inc(cleared, 1)
            eng.memset(selrow[:], 0.0).then_inc(cleared, 1)
            eng.memset(wS[:], 0.0).then_inc(cleared, 1)
            eng.wait_ge(cleared, 3)
            eng.wait_ge(loaded, 128)
            for n in range(2):
                for r in range(3):
                    eng.tensor_copy(bS[0:1, n, :, :, HD * (r + 1):HD * (r + 2)].rearrange("p g j c -> p (g j) c"),
                                    brow[0:1, n, :, :])
            eng.memset(bS[0:1, 1, :, :, 0:2], 1.0)
            eng.memset(selrow[0:1, 0, :, 3 * HD:4 * HD], 1.0)
            eng.memset(selrow[0:1, 1, :, 2 * HD:3 * HD], 1.0).then_inc(prep_dve, 1)
            eng.wait_ge(prep_pe, 1)
            eng.tensor_copy(wT[:, :, :].rearrange("p n c -> p (n c)"), MISC[:, :])
            for n in range(2):
                for r in range(3):
                    eng.tensor_copy(wS[:, n, :, :, HD * (r + 1):HD * (r + 2)].rearrange("p g j c -> p (g j) c"),
                                    MISC[:, n * P:n * P + P].rearrange("p (h c) -> p h c", c=HD))
            eng.wait_ge(prep_pe, 2)
            eng.tensor_copy(cols[:, :, :], PR[:, 0:16].rearrange("p (n c) -> p n c", n=2)[:, :, 0:G + 1])\
               .then_inc(prep_dve, 1)
            eng.wait_ge(prep_dve, 2)
            for n in range(2):
                last = eng.tensor_scalar(cols_s[:, n, :], cols[:, n, 0:G], cols[:, n, G:G + 1], None, ALU.mult)
            last.then_inc(prep_dve, 1)
            eng.wait_ge(prep_dve, 3)
            eng.wait_ge(prep_pool, 3)

            def projected(n, ring, k):
                gp, which = k // 2, k % 2
                dst = qs if which == 0 else ks
                eng.wait_ge(low_ready, n * 4 + k + 1)
                for gi in range(2):
                    g = 2 * gp + gi
                    out = eng.scalar_tensor_tensor(out=dst[:, ring, g, :], in0=PR[:, gi * T:gi * T + T],
                                                   scalar=cols[:, which, g:g + 1], in1=low[:, gi, :],
                                                   op0=ALU.add, op1=ALU.subtract)
                out.then_inc(proj_out, 1)

            def maxima(n, ring, u):
                gp, jp, t = u // 4, u % 4 // 2, u % 2
                nk = (t + 1) * P if causal else T
                eng.wait_ge(s_done, n * 8 + u + 1)
                eng.tensor_reduce(negmax[:, ring, t, 8 * gp:8 * gp + 8]
                                  .rearrange("p (a c b) -> p c b a", c=2, b=2)[:, jp, :, :],
                                  sh.banks[0][:, :].rearrange("p (b a k) -> p b a k", b=2, a=2)[:, :, :, 0:nk],
                                  AX.X, ALU.max, negate=True).then_inc(max_done, 1)

            def spread_maxima(n, ring, gp):
                hs = slice(8 * gp, 8 * gp + 8)
                eng.wait_ge(max_done, n * 8 + 4 * gp + 4)
                eng.tensor_copy(msp[:, ring, :, hs, 0:1].bitcast(F32R),
                                negmax[:, ring, :, hs].rearrange("p t (h a) -> p t h a", a=1))\
                   .then_inc(mhi_ready, 1)
                eng.wait_ge(mhi_ready, n * 2 + gp + 1)
                eng.tensor_tensor(msp[:, ring, :, hs, 1], negmax[:, ring, :, hs], msp[:, ring, :, hs, 0],
                                  ALU.subtract).then_inc(msp_ready, 1)

            def less_maxima(step, ring, gp):
                misc_filled(eng, step, f"mT{gp}")
                eng.tensor_tensor(qm[:, ring, 2 * gp:2 * gp + 2, :].rearrange("p g q -> p (g q)"), MISC[:, :],
                                  qs[:, ring, 2 * gp:2 * gp + 2, :].rearrange("p g q -> p (g q)").bitcast(F32),
                                  ALU.add).then_inc(misc_free, 1)

            def normalize(step, n, gp):
                misc_filled(eng, step, f"oT{gp}")
                o4 = MISC[:, :].rearrange("p (t g j c) -> p t (g j) c", t=NT, g=2, j=4)
                eng.reciprocal(rden[:, gp, :, :, :].rearrange("p t g j -> p t (g j)"), o4[:, :, :, HD])\
                   .then_inc(rden_ready, 1)
                eng.wait_ge(rden_ready, n * 2 + gp + 1)
                for t in range(NT):
                    out = eng.tensor_tensor(
                        ctxn[:, t, gp * 64:gp * 64 + 64].rearrange("p (h c) -> p h c", c=HD),
                        o4[:, t, :, 0:HD],
                        rden[:, gp, t, :, :].rearrange("p g (j a) -> p (g j) a", a=1).broadcast_to([P, 8, HD]),
                        ALU.mult)
                    out.then_inc(ctx_ready, 1)
                eng.wait_ge(ctx_ready, n * 4 + gp * 2 + 2)
                eng.sem_inc(misc_free, 1)

            def step(b, other):
                own = 1 - other
                for slot in range(8):
                    if has_front(b) and slot in PARTS:
                        projected(b + 1, other, PARTS.index(slot))
                    if has_front(b) and slot == 7:
                        less_maxima(b, other, 0)
                    if has_mid(b) and slot == 3:
                        less_maxima(b, own, 1)
                    if has_mid(b) and slot < 2:
                        maxima(b, own, slot + 6)
                        if slot == 1:
                            spread_maxima(b, own, 1)
                    if has_front(b) and slot >= 2:
                        maxima(b + 1, other, slot - 2)
                        if slot == 5:
                            spread_maxima(b + 1, other, 0)
                    if has_tail(b):
                        if slot == 2:
                            normalize(b, b - 1, 1)
                        if slot == 5:
                            misc_filled(eng, b, "wo")
                            eng.wait_ge(res_ready, b)
                            eng.tensor_tensor(y[:, :, :], MISC[:, 0:T].rearrange("p (t c) -> p t c", t=NT),
                                              x_res[:, other, :, :], ALU.add).then_inc(misc_free, 1)
                            misc_read(eng, b, "wo")
                            for t in range(NT):
                                st = eng.bn_stats(stats[:, t, :], y[:, t, :])
                            st.then_inc(stats_ready, 1)
                            eng.wait_ge(stats_ready, b)
                            apart(eng, sh)
                            for t in range(NT):
                                ag = eng.bn_aggr(mv[:, t, :], stats[:, t, :])
                            ag.then_inc(mv_ready, 1)
                        if slot == 7:
                            eng.wait_ge(rstd_ready, b)
                            for t in range(NT):
                                out = eng.tensor_scalar(sh.x[:, ds((b - 1) * NT + t, 1), :]
                                                        .rearrange("p a c -> p (a c)"), y[:, t, :],
                                                        mv[:, t, 0:1], rstd[:, t:t + 1],
                                                        ALU.subtract, ALU.mult)
                            out.then_inc(x_ready, 1)
                    if has_front(b) and slot == 1:
                        misc_filled(eng, b, "v")
                        for t in range(NT):
                            out = eng.tensor_tensor(va[:, other, t, :, 0:HD],
                                                    MISC[:, t * P:t * P + P].rearrange("p (h c) -> p h c", c=HD),
                                                    bvB[:, :].rearrange("p (h c) -> p h c", c=HD), ALU.add)
                        out.then_inc(misc_free, 1)
                    if has_mid(b) and slot == 6:
                        normalize(b, b, 0)

            steps(eng, step)
            eng.wait_ge(x_ready, B)


L = 2
FH = 8
FD = 64
INNER = FH * FD
HID = 341
HIDS = [128, 128, HID - 256]
BAND = 192
NORM2 = 2.0 ** 20
START = 1
MAX_INVERSE = 1e12 / 2.0 ** 10
TINY = 1e-30


class FfnMisc:

    FULL = ["hT", "wo", "xT", "mean", "var"]
    PER_LAYER = 5 * B

    @classmethod
    def before(cls, layer, step, use):
        if isinstance(step, int) and (step <= 0 or step >= B - 1):
            base = {-1: 0, 0: 1, B - 1: 5 * (B - 1) - 3, B: 5 * (B - 1) + 1}[step]
            at = 0 if step <= 0 else cls.FULL.index(use) - 1
            assert at >= 0 and (use == "hT") == (step <= 0)
            return layer * cls.PER_LAYER + (base + at)
        return layer * cls.PER_LAYER + step * 5 + (cls.FULL.index(use) - 3)


def ffn_stage(nc, sh, dram):
    (wqkv_d, qscale_d, kscale_d, wo_d, lng_d, lnb_d, w1_d, b1_d, w2_d, b2_d, rot_d, band_d, band0_d) = dram
    ctx = ExitStack()
    with ctx:
        def sb(what, shape, dt=F32):
            return ctx.enter_context(nc.sbuf_tensor(f"ffn_{what}", shape, dt))

        def sem(what):
            return sh.stack.enter_context(nc.semaphore(f"ffn_{what}"))

        rot_raw = sb("rot_raw", [P, 2, 2, T])
        band_raw = sb("band_raw", [P, BAND + P])
        band = sb("band", [P, BAND], BF16)
        band0 = sb("band0", [P, P], BF16)
        ones_head = sb("ones_head", [P, P])
        ones_mean = sb("ones_mean", [P, P])
        tiny = sb("tiny", [P, 1])

        wqkv = sb("wqkv", [P, 3 * INNER])
        wrot = sb("wrot", [P, 2 * FH, 2, 32])
        wo = sb("wo", [P, 4, P])
        w1 = sb("w1", [P, 2 * HID])
        w2 = sb("w2", [P, 3, P])
        b1 = sb("b1", [P, 6])
        b2B = sb("b2B", [P, P])
        lgb = sb("lgb", [P, 2])
        scol = sb("scol", [P, 2, 2])
        rot = sb("rot", [P, 2, 2, T])

        x_in = sb("x_in", [P, 2, NT, P])
        hT = sb("hT", [P, 2, T])
        squares = sb("squares", [P, 2, 2, T])
        turned = sb("turned", [P, 2, 2, T])
        sums = sb("sums", [P, 4, 2, T])
        capped = sb("capped", [P, 2 * T])
        logs = sb("logs", [P, 2 * T])
        inv = sb("inv", [P, 2, 2 * T])
        qk = sb("qk", [P, 2, 4, 2, T])
        v = sb("v", [P, 2, NT, INNER])
        UNIT_KEYS = [P, BAND]
        negmax = sb("negmax", [P, 2, FH, 2])
        den = sb("den", [P, 2, FH, 2])
        rden = sb("rden", [P, 2, FH, 2])
        raw = [sb("raw0", [P, 2, P]), sb("raw1", [P, 2, BAND])]
        probs = [sb("probs0", [P, 2, P]), sb("probs1", [P, 2, T])]
        probsT = [sb("probsT0", [P, 2, P]), sb("probsT1", [P, 2, T])]
        oT = sb("oT", [P, 4, T])
        x1 = sb("x1", [P, NT, P])
        h1T = sb("h1T", [P, T])
        cen = sb("cen", [P, T])
        cen2 = sb("cen2", [P, T])
        lnv = sb("lnv", [P, T])
        rstd = sb("rstd", [P, T])
        normed = sb("normed", [P, T])
        hn = sb("hn", [P, B * T])
        gate = sb("gate", [P, 3, 2 * T])
        hid = sb("hid", [P, 2, 3, 2 * T])

        PR, NV, S, PT, OT, MISC = (sh.bank[0], sh.bank[6]), sh.bank[1], sh.bank[2:4], sh.bank[4], sh.bank[5], sh.bank[7]

        const_in = sem("const_in")
        const_set = sem("const_set")
        pool_set = sem("pool_set")
        wa_in = sem("wa_in")
        wf_in = sem("wf_in")
        tables = sem("tables")
        x_copied = sem("x_copied")
        misc_done = sem("misc_done")
        misc_free = sem("misc_free")
        proj_done = sem("proj_done")
        squared = sem("squared")
        turned_ready = sem("turned_ready")
        summed = sem("summed")
        nv_done = sem("nv_done")
        nv_free = sem("nv_free")
        capped_ready = sem("capped_ready")
        log_ready = sem("log_ready")
        inv_ready = sem("inv_ready")
        qk_ready = sem("qk_ready")
        s_done = sem("s_done")
        max_done = sem("max_done")
        exp_done = sem("exp_done")
        rden_ready = sem("rden_ready")
        probs_ready = sem("probs_ready")
        pt_done = sem("pt_done")
        pt_out = sem("pt_out")
        pv_done = sem("pv_done")
        o_out = sem("o_out")
        res_ready = sem("res_ready")
        cen_ready = sem("cen_ready")
        cen2_ready = sem("cen2_ready")
        lnv_ready = sem("lnv_ready")
        rstd_ready = sem("rstd_ready")
        normed_ready = sem("normed_ready")
        hn_ready = sem("hn_ready")
        w1_done = sem("w1_done")
        gate_ready = sem("gate_ready")
        hid_ready = sem("hid_ready")
        w2_done = sem("w2_done")
        x_ready = sem("x_ready")

        counts = [cen2_ready, cen_ready, capped_ready, exp_done, gate_ready, hid_ready, hn_ready, inv_ready, log_ready, max_done, misc_done, misc_free, normed_ready, nv_done, nv_free, o_out, probs_ready, proj_done, pt_done, pt_out, pv_done, qk_ready, rden_ready, res_ready, rstd_ready, s_done, squared, summed, turned_ready, w1_done, w2_done, x_copied, x_ready]
        with nc.Block() as block:
            @block.gpsimd
            def _(eng):
                for count in counts:
                    eng.sem_inc(count, START)

        before = FfnMisc.before
        A_LOADS, F_LOADS = 14, 12
        NV_USES = 6

        def misc_begin(eng, l, step, use):
            eng.wait_ge(misc_free, START + before(l, step, use))

        def misc_filled(eng, l, step, use):
            eng.wait_ge(misc_done, START + before(l, step, use) + 1)

        def misc_read(eng, l, step, use):
            eng.wait_ge(misc_free, START + before(l, step, use) + 1)

        def steps(eng, l, body):
            body(l, -1, 0)
            body(l, 0, 1)
            with eng.Fori(0, (B - 2) // 2) as i:
                body(l, i * 2 + 1, 0)
                body(l, i * 2 + 2, 1)
            body(l, B - 1, 0)
            body(l, B, 1)

        def has_front(step):
            return not isinstance(step, int) or step < B - 1

        def has_mid(step):
            return not isinstance(step, int) or 0 <= step < B

        def has_tail(step):
            return not isinstance(step, int) or step > 0

        NORMS = {3: (0, 1), 5: (1, 3), 7: (2, 4)}

        block = ctx.enter_context(nc.Block())

        @block.sync
        def _(eng):
            eng.dma_start(rot_raw[:].rearrange("p a b t -> p (a b t)"), rot_d).then_inc(const_in, 16)
            eng.dma_start(band_raw[:, 0:BAND], band_d).then_inc(const_in, 16)
            eng.dma_start(band_raw[:, BAND:BAND + P], band0_d).then_inc(const_in, 16)
            with eng.Fori(0, L) as l:
                def row(d):
                    return d[ds(l, 1), :].rearrange("a n -> (a n)")

                def column(d, a, b):
                    return d[ds(l, 1), a:b].rearrange("a n -> n a")

                eng.wait_ge(hn_ready, START + l * B)
                apart(eng, sh)
                wl = wqkv_d[ds(l, 1), :, :].rearrange("a k n -> (a k) n")
                eng.dma_start(wqkv[:, :], wl).then_inc(wa_in, 16)
                eng.dma_start(wo[:, :, :], wo_d[ds(l, 1), :, :].rearrange("a (c p) n -> p (a c) n", p=P))\
                   .then_inc(wa_in, 16)
                for n, d in enumerate((qscale_d, kscale_d)):
                    for half in range(2):
                        p = half * FD
                        eng.dma_start(scol[p:p + FD, n, 0:1], column(d, 0, FD)).then_inc(wa_in, 16)
                        eng.dma_start(scol[p:p + 32, n, 1:2], column(d, 32, FD)).then_inc(wa_in, 16)
                        eng.dma_start(scol[p + 32:p + FD, n, 1:2], column(d, 0, 32)).then_inc(wa_in, 16)
                eng.wait_ge(x_ready, START + l * (B // 2))
                apart(eng, sh)
                eng.dma_start(lgb[:, 0:1], column(lng_d, 0, P)).then_inc(wf_in, 16)
                eng.dma_start(lgb[:, 1:2], column(lnb_d, 0, P)).then_inc(wf_in, 16)
                eng.dma_start(b2B[:, :], row(b2_d).partition_broadcast(P)).then_inc(wf_in, 16)
                eng.dma_start(w1[:, :], w1_d[ds(l, 1), :, :].rearrange("a k n -> (a k) n")).then_inc(wf_in, 16)
                for n in range(2):
                    for j in range(3):
                        at = n * HID + j * P
                        eng.dma_start(b1[0:HIDS[j], n * 3 + j:n * 3 + j + 1],
                                      column(b1_d, at, at + HIDS[j])).then_inc(wf_in, 16)
                w2l = w2_d[ds(l, 1), :, :].rearrange("a k n -> (a k) n")
                eng.dma_start(w2[:, 0:2, :], w2l[0:256, :].rearrange("(c p) n -> p c n", p=P)).then_inc(wf_in, 16)
                eng.dma_start(w2[0:HIDS[2], 2, :], w2l[256:HID, :]).then_inc(wf_in, 16)

        @block.gpsimd
        def _(eng):
            clears = [(probs[1][:, :, 0:T - BAND], 0.0), (ones_mean[:], 1.0 / P), (tiny[:], TINY), (ones_head[:], 0.0),
                      (ones_head[0:64, 0:64], 1.0), (ones_head[64:128, 64:128], 1.0),
                      (hT[64:128, :, 0:1], 0.0), (h1T[64:128, 0:1], 0.0)]
            for n, (where, value) in enumerate(clears):
                eng.wait_ge(pool_set, n)
                eng.memset(where, value).then_inc(pool_set, 1)
            eng.wait_ge(pool_set, len(clears))
            eng.wait_ge(const_in, 48)
            with eng.Fori(0, L) as l:
                eng.wait_ge(wa_in, (l + 1) * (16 * A_LOADS))
                apart(eng, sh)
                wq = wqkv[:, 0:2 * INNER].rearrange("p (g s d) -> p g s d", s=2, d=32)
                for s in range(2):
                    eng.tensor_scalar(wrot[:, :, s, :], wq[:, :, 1 - s, :], 1.0, None, ALU.mult).then_inc(tables, 1)
                for n in range(2):
                    for s in range(2):
                        eng.tensor_scalar(rot[:, n, s, :], rot_raw[:, n, s, :], scol[:, n, s:s + 1], None,
                                          ALU.mult).then_inc(tables, 1)

                def add(n, c):
                    eng.wait_ge(turned_ready, START + (l * B + n) * 8 + c + 1)
                    eng.tensor_tensor(sums[:, c // 2, c % 2, :], turned[:, c % 2, 0, :], turned[:, c % 2, 1, :],
                                      ALU.add).then_inc(summed, 1)

                def scale(n, ring, i):
                    eng.wait_ge(inv_ready, START + (l * B + n) * 4 + i + 1)
                    eng.wait_ge(summed, START + (l * B + n) * 8 + 2 * i + 2)
                    eng.wait_ge(qk_ready, START + (l * B + n) * 4 + i)
                    apart(eng, sh)
                    eng.tensor_scalar(capped[:, :], inv[:, i % 2, :], MAX_INVERSE, None, ALU.min)\
                       .then_inc(capped_ready, 1)
                    eng.wait_ge(capped_ready, START + (l * B + n) * 4 + i + 1)
                    apart(eng, sh)
                    eng.tensor_tensor(qk[:, ring, i, :, :].rearrange("p a t -> p (a t)"),
                                      sums[:, i, :, :].rearrange("p a t -> p (a t)"), capped[:, :],
                                      ALU.mult).then_inc(qk_ready, 1)

                def step(l, b, other):
                    own = 1 - other
                    for slot in range(8):
                        if has_mid(b) and slot == 0:
                            scale(b, own, 2)
                            add(b, 7)
                        if has_front(b) and slot >= 1:
                            add(b + 1, slot - 1)
                        if has_mid(b) and slot == 2:
                            scale(b, own, 3)
                        if has_front(b) and slot == 4:
                            scale(b + 1, other, 0)
                        if has_front(b) and slot == 6:
                            scale(b + 1, other, 1)
                        if has_tail(b) and slot == 5:
                            misc_read(eng, l, b, "wo")
                            if not isinstance(b, int) or b == 1:
                                eng.wait_ge(wf_in, (l + 1) * (16 * F_LOADS))
                            for t in range(NT):
                                out = eng.tensor_tensor(sh.x[:, ds((b - 1) * NT + t, 1), :]
                                                        .rearrange("p a c -> p (a c)"), x1[:, t, :], b2B[:, :],
                                                        ALU.add)
                            out.then_inc(res_ready, 1)

                steps(eng, l, step)

        @block.tensor
        def _(eng):
            eng.wait_ge(pool_set, 8)
            eng.wait_ge(const_set, 1)
            with eng.Fori(0, L) as l:
                eng.wait_ge(wa_in, (l + 1) * (16 * A_LOADS))
                eng.wait_ge(tables, (l + 1) * 6)

                def project(n, ring, c):
                    i, which = c // 2, c % 2
                    if c == 0:
                        misc_read(eng, l, n - 1, "hT")
                    eng.wait_ge(turned_ready, START + (l * B + n) * 8 + max(c - 1, 0))
                    at = which * INNER + i * P
                    eng.matmul(PR[c % 2][:, 0:T], wqkv[:, at:at + P], hT[:, ring, :], start=True, stop=True)
                    eng.matmul(PR[c % 2][:, T:2 * T],
                               wrot[:, at // FD:at // FD + 2, :, :].rearrange("p g s d -> p (g s d)"),
                               hT[:, ring, :], start=True, stop=True).then_inc(proj_done, 1)

                def norms(n, i, nth):
                    eng.wait_ge(squared, START + (l * B + n) * 8 + 2 * i + 2)
                    eng.wait_ge(nv_free, START + (l * B + n) * NV_USES + nth)
                    eng.matmul(NV[:, :], ones_head[:, :], squares[:, i % 2, :, :].rearrange("p a t -> p (a t)"),
                               start=True, stop=True).then_inc(nv_done, 1)

                def values_in(n, ring, t, nth):
                    eng.wait_ge(nv_free, START + (l * B + n) * NV_USES + nth)
                    eng.matmul(NV[:, :], hT[:, ring, t * P:t * P + P], wqkv[:, 2 * INNER:3 * INNER],
                               start=True, stop=True).then_inc(nv_done, 1)

                def scores(n, ring, u):
                    i, t = u // 2, u % 2
                    w = UNIT_KEYS[t]
                    if t == 0:
                        eng.wait_ge(qk_ready, START + (l * B + n) * 4 + i + 1)
                    eng.wait_ge(exp_done, START + (l * B + n) * 8 + u)
                    for hb in range(2):
                        p = 64 * hb
                        eng.matmul(S[hb][:, 0:w], qk[p:p + 64, ring, i, 0, t * P:t * P + P],
                                   qk[p:p + 64, ring, i, 1, (t + 1) * P - w:(t + 1) * P], start=True, stop=False)
                    for hb in range(2):
                        mm = eng.matmul(S[hb][:, 0:w], sh.ident_b[:, :], (band0, band)[t][:, :], start=False,
                                        stop=True)
                    mm.then_inc(s_done, 1)

                def prob_transposes(n, u):
                    t = u % 2
                    eng.wait_ge(probs_ready, START + (l * B + n) * 8 + u + 1)
                    eng.wait_ge(pt_out, START + (l * B + n) * 8 + u)
                    for k in range(2 * (t + 1)):
                        tr = eng.transpose(PT[:, k * P:k * P + P],
                                           probs[t][:, :, :].rearrange("p h k -> p (h k)")[:, k * P:k * P + P],
                                           sh.ident[:, :])
                    tr.then_inc(pt_done, 1)

                def values(n, ring, u):
                    i, t = u // 2, u % 2
                    eng.wait_ge(pt_out, START + (l * B + n) * 8 + u + 1)
                    if u % 4 == 0:
                        eng.wait_ge(o_out, START + (l * B + n) * 2 + u // 4)
                    for k in range(t + 1):
                        for hb in range(2):
                            p, h = 64 * hb, 2 * i + hb
                            mm = eng.matmul(OT[p:p + 64, (i % 2) * T + t * P:(i % 2) * T + t * P + P],
                                            v[:, ring, k, h * FD:h * FD + FD], probsT[t][:, hb, k * P:k * P + P],
                                            start=(k == 0), stop=(k == t))
                    mm.then_inc(pv_done, 1)

                def step(l, b, other):
                    own = 1 - other
                    for slot in range(8):
                        if has_mid(b):
                            scores(b, own, slot)
                            if slot == 0:
                                project(b, own, 7)
                            if slot == 1:
                                norms(b, 3, 5)
                        if has_front(b):
                            if slot >= 1:
                                project(b + 1, other, slot - 1)
                            if slot == 2:
                                values_in(b + 1, other, 0, 0)
                            if slot == 3:
                                norms(b + 1, 0, 1)
                            if slot == 4:
                                values_in(b + 1, other, 1, 2)
                            if slot == 5:
                                norms(b + 1, 1, 3)
                            if slot == 7:
                                norms(b + 1, 2, 4)
                        if has_mid(b) and slot >= 1:
                            prob_transposes(b, slot - 1)
                            if slot >= 2:
                                values(b, own, slot - 2)
                        if has_tail(b):
                            if slot == 0:
                                prob_transposes(b - 1, 7)
                                values(b - 1, other, 6)
                            if slot == 1:
                                values(b - 1, other, 7)
                        if has_front(b) and slot == 0:
                            misc_begin(eng, l, b, "hT")
                            eng.wait_ge(x_copied, START + l * B + b + 2)
                            for t in range(NT):
                                tr = eng.transpose(MISC[:, t * P:t * P + P], x_in[:, other, t, :], sh.ident[:, :])
                            tr.then_inc(misc_done, 1)
                        if has_tail(b):
                            if slot == 2:
                                misc_begin(eng, l, b, "wo")
                                eng.wait_ge(o_out, START + (l * B + b) * 2)
                                for t in range(NT):
                                    for c in range(4):
                                        mm = eng.matmul(MISC[:, t * P:t * P + P], oT[:, c, t * P:t * P + P],
                                                        wo[:, c, :], start=(c == 0), stop=(c == 3))
                                mm.then_inc(misc_done, 1)
                            if slot == 3:
                                misc_begin(eng, l, b, "xT")
                                for t in range(NT):
                                    tr = eng.transpose(MISC[:, t * P:t * P + P], x1[:, t, :], sh.ident[:, :])
                                tr.then_inc(misc_done, 1)
                            if slot == 4:
                                misc_begin(eng, l, b, "mean")
                                eng.matmul(MISC[:, 0:T], ones_mean[:, :], h1T[:, :], start=True, stop=True)\
                                   .then_inc(misc_done, 1)
                            if slot == 6:
                                misc_begin(eng, l, b, "var")
                                eng.wait_ge(cen2_ready, START + l * B + b)
                                eng.matmul(MISC[:, 0:T], ones_mean[:, :], cen2[:, :], start=True, stop=True)\
                                   .then_inc(misc_done, 1)

                steps(eng, l, step)

                eng.wait_ge(wf_in, (l + 1) * (16 * F_LOADS))
                eng.wait_ge(hn_ready, START + (l + 1) * B)

                def up(m, place):
                    for j in range(3):
                        eng.wait_ge(hid_ready, START + (l * 4 + m) * 3)
                        for n in range(2):
                            at = n * HID + j * P
                            mm = eng.matmul(sh.bank[2 * j + n][0:HIDS[j], :], w1[:, at:at + HIDS[j]],
                                            hn[:, ds(m * (2 * T), 2 * T)], start=True, stop=True)
                        mm.then_inc(w1_done, 1)

                def down(m, place):
                    eng.wait_ge(hid_ready, START + (l * 4 + m) * 3 + 3)
                    eng.wait_ge(x_ready, START + l * 4 + m)
                    for t in range(4):
                        for j in range(3):
                            mm = eng.matmul(sh.bank[6 + place][:, t * P:t * P + P],
                                            hid[0:HIDS[j], place, j, t * P:t * P + P], w2[0:HIDS[j], j, :],
                                            start=(j == 0), stop=(j == 2))
                    mm.then_inc(w2_done, 1)

                up(0, 0)
                with eng.Fori(0, 1) as i:
                    up(i * 2 + 1, 1)
                    down(i * 2, 0)
                    up(i * 2 + 2, 0)
                    down(i * 2 + 1, 1)
                up(3, 1)
                down(2, 0)
                down(3, 1)

        @block.scalar
        def _(eng):
            eng.wait_ge(pool_set, 8)
            with eng.Fori(0, L) as l:
                eng.preload_act_table_set("natural_log_exp_and_others")

                def shifted(dst, out_sem):
                    eng.activation(dst[0:64, 0:T], MISC[0:64, 0:T], ACT.Copy)
                    eng.activation(dst[64:128, 1:T], MISC[64:128, 0:T - 1], ACT.Copy).then_inc(out_sem, 1)

                def inverses(n, i, nth):
                    N = l * B + n
                    eng.wait_ge(nv_done, START + N * NV_USES + nth + 1)
                    eng.wait_ge(inv_ready, START + N * 4 + i)
                    eng.activation(logs[:, :], NV[:, :], ACT.Ln, scale=NORM2, bias=tiny[:, 0:1]).then_inc(log_ready, 1)
                    eng.wait_ge(log_ready, START + N * 4 + i + 1)
                    eng.sem_inc(nv_free, 1)
                    eng.wait_ge(qk_ready, START + N * 4 + max(i - 1, 0))
                    eng.activation(inv[:, i % 2, :], logs[:, :], ACT.Exp, scale=-0.5).then_inc(inv_ready, 1)

                def exps(n, ring, u):
                    eng.wait_ge(max_done, START + (l * B + n) * 8 + u + 1)
                    eng.wait_ge(probs_ready, START + (l * B + n) * 8 + max(u - 1, 0))
                    for hb in range(2):
                        ex = eng.activation(raw[u % 2][:, hb, :], S[hb][:, 0:UNIT_KEYS[u % 2]], ACT.Exp,
                                            bias=negmax[:, ring, u, hb:hb + 1],
                                            accum_out=den[:, ring, u, hb:hb + 1])
                    ex.then_inc(exp_done, 1)

                def evac_out(n, half):
                    eng.wait_ge(pv_done, START + (l * B + n) * 8 + 4 * half + 4)
                    eng.activation(oT[:, 2 * half:2 * half + 2, :].rearrange("p c t -> p (c t)"), OT[:, :],
                                   ACT.Copy).then_inc(o_out, 1)

                def square(n, c):
                    eng.wait_ge(proj_done, START + (l * B + n) * 8 + c + 1)
                    eng.activation(squares[:, (c // 2) % 2, c % 2, :], PR[c % 2][:, 0:T],
                                   ACT.Square).then_inc(squared, 1)

                def step(l, b, other):
                    own = 1 - other
                    for slot in range(8):
                        if has_mid(b):
                            exps(b, own, slot)
                            if slot == 0:
                                square(b, 7)
                            if slot == 1:
                                inverses(b, 3, 5)
                        if has_front(b):
                            if slot == 0:
                                misc_filled(eng, l, b, "hT")
                                shifted(hT[:, other, :], misc_free)
                            if slot >= 1:
                                square(b + 1, slot - 1)
                            if slot in (2, 4):
                                t = slot // 2 - 1
                                eng.wait_ge(nv_done, START + (l * B + b + 1) * NV_USES + 2 * t + 1)
                                eng.activation(v[:, other, t, :], NV[:, :], ACT.Copy).then_inc(nv_free, 1)
                            if slot in NORMS:
                                inverses(b + 1, *NORMS[slot])
                        if has_tail(b):
                            if slot == 3:
                                misc_filled(eng, l, b, "xT")
                                shifted(h1T, misc_free)
                            if slot == 4:
                                eng.wait_ge(cen_ready, START + l * B + b)
                                eng.activation(cen2[:, :], cen[:, :], ACT.Square).then_inc(cen2_ready, 1)
                            if slot == 6:
                                misc_filled(eng, l, b, "var")
                                eng.activation(lnv[:, :], MISC[:, 0:T], ACT.Ln, bias=sh.eps[:, 0:1])\
                                   .then_inc(misc_free, 1)
                                misc_read(eng, l, b, "var")
                                eng.activation(rstd[:, :], lnv[:, :], ACT.Exp, scale=-0.5).then_inc(rstd_ready, 1)
                            if slot == 1:
                                evac_out(b - 1, 1)
                        if has_mid(b) and slot == 5:
                            evac_out(b, 0)

                steps(eng, l, step)
                eng.preload_act_table_set("gelu_and_others")
                eng.wait_ge(wf_in, (l + 1) * (16 * F_LOADS))
                with eng.Fori(0, 4) as m:
                    for j in range(3):
                        eng.wait_ge(w1_done, START + (l * 4 + m) * 3 + j + 1)
                        eng.wait_ge(hid_ready, START + (l * 4 + m) * 3)
                        eng.activation(gate[0:HIDS[j], j, :], sh.bank[2 * j + 1][0:HIDS[j], :], ACT.Gelu,
                                       bias=b1[0:HIDS[j], 3 + j:4 + j]).then_inc(gate_ready, 1)

        @block.vector
        def _(eng):
            eng.wait_ge(const_in, 48)
            eng.tensor_copy(band[:, :], band_raw[:, 0:BAND])
            eng.tensor_copy(band0[:, :], band_raw[:, BAND:BAND + P]).then_inc(const_set, 1)
            eng.wait_ge(pool_set, 8)
            with eng.Fori(0, L) as l:
                eng.wait_ge(tables, (l + 1) * 6)

                def turn(n, c):
                    i, which = c // 2, c % 2
                    N = l * B + n
                    eng.wait_ge(squared, START + N * 8 + c + 1)
                    eng.wait_ge(summed, START + N * 8 + max(c - 1, 0))
                    eng.tensor_tensor(turned[:, c % 2, :, :].rearrange("p a t -> p (a t)"), PR[c % 2][:, :],
                                      rot[:, which, :, :].rearrange("p a t -> p (a t)"),
                                      ALU.mult).then_inc(turned_ready, 1)

                def maxima(n, ring, u):
                    eng.wait_ge(s_done, START + (l * B + n) * 8 + u + 1)
                    eng.tensor_reduce(negmax[:, ring, u, :],
                                      sh.banks[1][:, :].rearrange("p (h k) -> p h k", h=2)[:, :, 0:UNIT_KEYS[u % 2]],
                                      AX.X, ALU.max, negate=True).then_inc(max_done, 1)

                def normalize(n, ring, u):
                    N = l * B + n
                    eng.wait_ge(exp_done, START + N * 8 + u + 1)
                    eng.reciprocal(rden[:, ring, u, :], den[:, ring, u, :]).then_inc(rden_ready, 1)
                    eng.wait_ge(rden_ready, START + N * 8 + u + 1)
                    eng.wait_ge(pt_done, START + N * 8 + max(u - 1, 0))
                    at = (0, T - BAND)[u % 2]
                    for hb in range(2):
                        out = eng.tensor_scalar(probs[u % 2][:, hb, at:at + UNIT_KEYS[u % 2]], raw[u % 2][:, hb, :],
                                                rden[:, ring, u, hb:hb + 1], None, ALU.mult)
                    out.then_inc(probs_ready, 1)

                def evac_T(n, u):
                    eng.wait_ge(pt_done, START + (l * B + n) * 8 + u + 1)
                    eng.tensor_copy(probsT[u % 2][:, :, :].rearrange("p h k -> p (h k)"),
                                    PT[:, 0:2 * P * (u % 2 + 1)]).then_inc(pt_out, 1)

                def copy_in(n, ring):
                    if not (isinstance(n, int) and n < 2):
                        eng.wait_ge(proj_done, START + (l * B + n - 2) * 8 + 1)
                    eng.tensor_scalar(x_in[:, ring, :, :], sh.x[:, ds(n * NT, NT), :], 1.0, None, ALU.mult)\
                       .then_inc(x_copied, 1)

                def step(l, b, other):
                    own = 1 - other
                    for slot in range(8):
                        if has_front(b) and slot == 0:
                            copy_in(b + 1, other)
                        if has_tail(b) and slot == 0:
                            normalize(b - 1, other, 7)
                        if has_mid(b) and slot >= 1:
                            normalize(b, own, slot - 1)
                        if has_mid(b):
                            maxima(b, own, slot)
                        if has_tail(b) and slot < 2:
                            evac_T(b - 1, slot + 6)
                        if has_mid(b) and slot >= 2:
                            evac_T(b, slot - 2)
                        if has_mid(b):
                            if slot == 0:
                                turn(b, 7)
                        if has_tail(b):
                            if slot == 2:
                                misc_filled(eng, l, b, "wo")
                                eng.wait_ge(res_ready, START + l * B + b - 1)
                                for t in range(NT):
                                    out = eng.tensor_tensor(x1[:, t, :], MISC[:, t * P:t * P + P],
                                                            sh.x[:, ds((b - 1) * NT + t, 1), :]
                                                            .rearrange("p a c -> p (a c)"), ALU.add)
                                out.then_inc(misc_free, 1)
                            if slot == 4:
                                misc_filled(eng, l, b, "mean")
                                eng.tensor_tensor(cen[:, :], h1T[:, :], MISC[:, 0:T], ALU.subtract)\
                                   .then_inc(cen_ready, 1)
                                eng.wait_ge(cen_ready, START + l * B + b)
                                eng.sem_inc(misc_free, 1)
                            if slot == 7:
                                eng.wait_ge(rstd_ready, START + l * B + b)
                                eng.tensor_tensor(normed[:, :], cen[:, :], rstd[:, :], ALU.mult)\
                                   .then_inc(normed_ready, 1)
                                eng.wait_ge(normed_ready, START + l * B + b)
                                eng.wait_ge(wf_in, (l + 1) * (16 * F_LOADS))
                                eng.tensor_scalar(hn[:, ds((b - 1) * T, T)], normed[:, :], lgb[:, 0:1],
                                                  lgb[:, 1:2], ALU.mult, ALU.add).then_inc(hn_ready, 1)
                        if has_front(b):
                            if slot >= 1:
                                turn(b + 1, slot - 1)

                steps(eng, l, step)

                with eng.Fori(0, 2) as i:
                    for place in range(2):
                        M = l * 4 + i * 2 + place
                        for j in range(3):
                            eng.wait_ge(gate_ready, START + M * 3 + j + 1)
                            eng.scalar_tensor_tensor(out=hid[0:HIDS[j], place, j, :],
                                                     in0=sh.bank[2 * j][0:HIDS[j], :],
                                                     scalar=b1[0:HIDS[j], j:j + 1], in1=gate[0:HIDS[j], j, :],
                                                     op0=ALU.add, op1=ALU.mult).then_inc(hid_ready, 1)
                        eng.wait_ge(w2_done, START + M + 1)
                        eng.wait_ge(res_ready, START + (l + 1) * B)
                        xs = sh.x[:, ds((i * 2 + place) * 4, 4), :].rearrange("p a c -> p (a c)")
                        eng.tensor_tensor(xs, xs, sh.bank[6 + place][:, :], ALU.add).then_inc(x_ready, 1)
            eng.wait_ge(x_ready, START + 8)


def final_stage(nc, sh, out_d):
    ctx = ExitStack()
    with ctx:
        def sb(what, shape, dt=F32):
            return ctx.enter_context(nc.sbuf_tensor(f"last_{what}", shape, dt))

        def sem(what):
            return sh.stack.enter_context(nc.semaphore(f"last_{what}"))

        N = B * NT
        y = sb("y", [P, N, P])
        out = sb("out", [P, N, P])
        stats = sb("stats", [P, N, 6])
        mv = sb("mv", [P, N, 2])
        lnv = sb("lnv", [P, N])
        rstd = sb("rstd", [P, N])
        summed, measured, aggregated, logged, rooted, scaled, stored = (
            sem(w) for w in ("summed", "measured", "aggregated", "logged", "rooted", "scaled", "stored"))
        block = ctx.enter_context(nc.Block())

        @block.vector
        def _(eng):
            for q in range(2):
                a, b = q * N // 2, (q + 1) * N // 2
                eng.tensor_tensor(y[:, a:b, :], sh.x0[:, a:b, :], sh.x[:, a:b, :], ALU.add).then_inc(summed, 1)
            for n in range(N):
                if n % (N // 2) == 0:
                    eng.wait_ge(summed, n // (N // 2) + 1)
                eng.bn_stats(stats[:, n, :], y[:, n, :]).then_inc(measured, 1)
            for n in range(N):
                eng.wait_ge(measured, n + 1)
                eng.bn_aggr(mv[:, n, :], stats[:, n, :]).then_inc(aggregated, 1)
            eng.wait_ge(rooted, 1)
            for n in range(N):
                eng.tensor_scalar(out[:, n, :], y[:, n, :], mv[:, n, 0:1], rstd[:, n:n + 1], ALU.subtract,
                                  ALU.mult).then_inc(scaled, 1)

        @block.scalar
        def _(eng):
            eng.preload_act_table_set("natural_log_exp_and_others")
            eng.wait_ge(aggregated, N)
            eng.activation(lnv[:, :], mv[:, :, 1], ACT.Ln, bias=sh.eps[:, 0:1]).then_inc(logged, 1)
            eng.wait_ge(logged, 1)
            eng.activation(rstd[:, :], lnv[:, :], ACT.Exp, scale=-0.5).then_inc(rooted, 1)

        @block.sync
        def _(eng):
            for q in range(4):
                a, b = q * N // 4, (q + 1) * N // 4
                eng.wait_ge(scaled, b)
                eng.dma_start(out_d[:, a:b, :], out[:, a:b, :]).then_inc(stored, 16)
            eng.wait_ge(stored, 64)


def build(nc, args, out):
    x_d = args["x"].rearrange("b (t p) d -> p (b t) d", p=P)
    ctx_d = args["ctx_1024"].rearrange("b (t p) d -> p (b t) d", p=P)
    out_d = out.rearrange("b (t p) d -> p (b t) d", p=P)
    sh = Shared()
    stack = ExitStack()
    sh.stack = stack
    with stack:
        def sb(name, shape, dt=F32):
            return stack.enter_context(nc.sbuf_tensor(name, shape, dt))

        sh.x = sb("x_all", [P, B * NT, P])
        sh.x0 = sb("x0", [P, B * NT, P])
        sh.ident = sb("ident", [P, P])
        sh.ident_b = sb("ident_b", [P, P], BF16)
        sh.causal = sb("causal", [P, P], BF16)
        sh.causal_T = sb("causal_T", [P, P], BF16)
        sh.one = sb("one", [1, 1])
        sh.eps = sb("eps", [P, 1])
        cm = sb("causal_raw", [P, 2, P])
        sh.banks = [stack.enter_context(nc.psum_tensor(f"banks{i}", [P, 2 * 512], F32)) for i in range(4)]
        sh.bank = [sh.banks[i // 2][:, (i % 2) * 512:(i % 2) * 512 + 512] for i in range(8)]
        const_loaded = stack.enter_context(nc.semaphore("const_loaded"))
        const_ready = stack.enter_context(nc.semaphore("const_ready"))
        sh.passed = stack.enter_context(nc.semaphore("passed"))
        stored = stack.enter_context(nc.semaphore("stored"))
        with nc.Block() as block:
            @block.sync
            def _(eng):
                eng.dma_start(sh.ident[:, :], args["c_ident"]).then_inc(const_loaded, 16)
                eng.dma_start(cm[:, 0, :], args["c_causal"]).then_inc(const_loaded, 16)
                eng.dma_start(cm[:, 1, :], args["c_causal_T"]).then_inc(const_loaded, 16)

            @block.vector
            def _(eng):
                eng.memset(sh.one[:, :], 1.0)
                eng.memset(sh.eps[:, :], EPS)
                eng.wait_ge(const_loaded, 48)
                eng.tensor_copy(sh.ident_b[:, :], sh.ident[:, :])
                eng.tensor_copy(sh.causal[:, :], cm[:, 0, :])
                eng.tensor_copy(sh.causal_T[:, :], cm[:, 1, :]).then_inc(const_ready, 1)

        for name, causal, cd in (("self", True, None), ("cross", False, ctx_d)):
            if name not in STAGES:
                continue
            p = "L0_attn_" if name == "self" else "L0_xattn_"
            attention_stage(nc, sh, name, causal, [args[p + k] for k in ("Wq", "Wk", "Wv", "Wo", "bq", "bk", "bv", "bo")],
                            x_d, cd)

        if "ffn" in STAGES:
            kept = stack.enter_context(nc.semaphore("kept"))
            if len(STAGES) == 1:
                with nc.Block() as block:
                    @block.sync
                    def _(eng):
                        eng.dma_start(sh.x[:, :, :], x_d).then_inc(const_loaded, 16)
                        eng.wait_ge(const_loaded, 64)
            with nc.Block() as block:
                @block.gpsimd
                def _(eng):
                    eng.tensor_scalar(sh.x0[:, :, :], sh.x[:, :, :], 1.0, None, ALU.mult).then_inc(kept, 1)
                    eng.wait_ge(kept, 1)
            f = "L0_ffn_"
            ffn_stage(nc, sh, [args[f + k] for k in ("wqkv", "q_scale", "k_scale", "wo", "ln_g", "ln_b", "w1", "b1",
                                                     "w2", "b2")] + [args["c_rot"], args["c_band"], args["c_band0"]])
            final_stage(nc, sh, out_d)
            return
        with nc.Block() as block:
            @block.sync
            def _(eng):
                eng.dma_start(out_d, sh.x[:, :, :]).then_inc(stored, 16)
                eng.wait_ge(stored, 16)


NEG = -1e30


def host_constants(np):
    i = np.arange(P)
    causal = np.where(i[None, :] <= i[:, None], 0, NEG).astype(np.float32)
    gap = np.arange(BAND)[None, :] - i[:, None]
    band = np.where((gap >= 0) & (gap <= 64), 0, NEG).astype(np.float32)
    gap0 = i[:, None] - i[None, :]
    band0 = np.where((gap0 >= 0) & (gap0 <= 64), 0, NEG).astype(np.float32)
    half = np.arange(0, FD, 2, dtype=np.float32)
    inv_freq = (1.0 / np.power(np.float32(10000.0), half / np.float32(FD))).astype(np.float32)
    t = np.arange(T, dtype=np.float32)
    freqs = np.concatenate([t[:, None] * inv_freq[None, :]] * 2, axis=-1)
    base = ((half + np.float32(0.4 * FD)) / np.float32(1.4 * FD)).astype(np.float32)
    power = (t - T // 2) / np.float32(32.0)
    scale = np.power(base[None, :], power[:, None]).astype(np.float32)
    scale = np.concatenate([scale, scale], axis=-1)
    cos, sin = np.cos(freqs), np.sin(freqs)
    sign = np.where(np.arange(FD) < FD // 2, -1.0, 1.0).astype(np.float32)[None, :]
    root = np.float32(NORM2 ** 0.5)
    rot = np.zeros((2, 2, FD, T), np.float32)
    rot[0, 0] = (cos * scale).T * (8 * root)
    rot[0, 1] = (sign * sin * scale).T * (8 * root)
    rot[1, 0] = (cos / scale).T * root
    rot[1, 1] = (sign * sin / scale).T * root
    rot = np.concatenate([rot, rot], axis=2).transpose(2, 0, 1, 3).reshape(P, 4 * T)
    return {"c_ident": np.eye(P, dtype=np.float32), "c_causal": causal, "c_causal_T": np.ascontiguousarray(causal.T),
            "c_rot": np.ascontiguousarray(rot.astype(np.float32)), "c_band": band, "c_band0": band0}




def kernel(**inputs):
    import numpy as np
    import concourse.bacc as bacc
    from concourse.bass_utils import run_bass_kernel_spmd as run

    nc = bacc.Bacc("TRN2", target_bir_lowering=False, num_devices=1)
    arrays, args = {}, {}
    for name, a in list(inputs.items()) + list(host_constants(np).items()):
        a = np.ascontiguousarray(a)
        arrays[f"in_{name}_dram"] = a
        args[name] = nc.dram_tensor(f"in_{name}_dram", a.shape, mybir.dt.from_np(a.dtype), kind="ExternalInput").ap()
    out = nc.dram_tensor("out_0_dram", (B, T, P), F32, kind="ExternalOutput").ap()
    build(nc, args, out)
    r = run(nc, [arrays], core_ids=[0])
    return r.results[0]["out_0_dram"]
```

```python
from contextlib import ExitStack

import concourse.bass as bass
from concourse import mybir

F32 = mybir.dt.float32
F32R = mybir.dt.float32r
BF16 = mybir.dt.bfloat16
ALU = mybir.AluOpType
ACT = mybir.ActivationFunctionType
AX = mybir.AxisListType

P = 128
B = 8
T = 256
NT = T // P
H = 16
HD = 8
G = H // 4
EPS = 1e-5
SM_SCALE = float(1.0 / (HD ** 0.5))


def ds(start, size):
    return bass.ds(start, size)


class Shared:
    pass


def apart(eng, sh):
    eng.sem_inc(sh.passed, 1)


class AttnMisc:

    FULL = ["xT", "v", "oT1", "mT1", "cT", "wo", "oT0", "mT0"]
    FIRST = {-1: ["xT", "v", "mT0"], 0: ["xT", "v", "mT1", "oT0", "mT0"],
             B - 1: ["oT1", "mT1", "cT", "wo", "oT0"], B: ["oT1", "cT", "wo"]}

    @classmethod
    def before(cls, step, use):
        if isinstance(step, int) and step in cls.FIRST:
            base = {-1: 0, 0: 3, B - 1: 8 * (B - 1), B: 8 * (B - 1) + 5}[step]
            return base + cls.FIRST[step].index(use)
        return step * 8 + cls.FULL.index(use)


class AttnWeights:

    LOADS = 8

    def __init__(self, sb, sem, dram, banks):
        self.dram, self.banks = dram, banks
        self.w_raw = sb("w_raw", [P, 4, P])
        self.wT = sb("wT", [P, 4, P])
        self.wS = sb("wS", [P, 2, G, 4, 32])
        self.brow = sb("brow", [G, 2, 4, HD])
        self.bS = sb("bS", [G, 2, 4, 32])
        self.selrow = sb("selrow", [1, 2, 4, 32])
        self.cols = sb("cols", [P, 2, G + 1])
        self.cols_s = sb("cols_s", [P, 2, G])
        self.bvB = sb("bvB", [P, P])
        self.boB = sb("boB", [P, P])
        self.loaded = sem("loaded")
        self.cleared = sem("cleared")
        self.rows_ready = sem("rows_ready")
        self.transposed = sem("transposed")
        self.columns_done = sem("columns_done")
        self.columns_out = sem("columns_out")

    def load(self, eng):
        Wq, Wk, Wv, Wo, bq, bk, bv, bo = self.dram
        for n, w in enumerate((Wq, Wk, Wv, Wo)):
            eng.dma_start(self.w_raw[:, n, :], w).then_inc(self.loaded, 16)
        for n, b in enumerate((bq, bk)):
            eng.dma_start(self.brow[:, n, :, :], b.rearrange("(g j d) -> g j d", g=G, d=HD))\
               .then_inc(self.loaded, 16)
        eng.dma_start(self.bvB[:, :], bv.partition_broadcast(P)).then_inc(self.loaded, 16)
        eng.dma_start(self.boB[:, :], bo.partition_broadcast(P)).then_inc(self.loaded, 16)

    def transpose(self, eng, sh):
        for_weights, for_columns = self.banks
        eng.wait_ge(self.loaded, 16 * self.LOADS)
        for n in range(4):
            tr = eng.transpose(for_weights[:, n * P:n * P + P], self.w_raw[:, n, :], sh.ident[:, :])
        tr.then_inc(self.transposed, 1)
        eng.wait_ge(self.rows_ready, 1)
        for n in range(2):
            eng.transpose(for_columns[:, n * 8:n * 8 + G], self.bS[:, n, :, :].rearrange("p j c -> p (j c)"),
                          sh.ident[0:G, 0:G])
            mm = eng.matmul(for_columns[:, n * 8 + G:n * 8 + G + 1],
                            self.selrow[0:1, n, :, :].rearrange("p j c -> p (j c)"), sh.one[0:1, 0:1],
                            start=True, stop=True)
        mm.then_inc(self.columns_done, 1)

    def clear(self, eng):
        eng.memset(self.bS[:], 0.0).then_inc(self.cleared, 1)
        eng.memset(self.selrow[:], 0.0).then_inc(self.cleared, 1)
        eng.memset(self.wS[:], 0.0).then_inc(self.cleared, 1)

    def lay_rows(self, eng):
        bS, selrow = self.bS, self.selrow
        eng.wait_ge(self.cleared, 3)
        eng.wait_ge(self.loaded, 16 * self.LOADS)
        for r in range(3):
            eng.tensor_copy(bS[:, :, :, HD * (r + 1):HD * (r + 2)].rearrange("p n j c -> p (n j) c"),
                            self.brow[:, :, :, :].rearrange("p n j c -> p (n j) c"))
        eng.memset(bS[:, 1, :, 0:2], 1.0)
        eng.memset(selrow[0:1, 0, :, 3 * HD:4 * HD], 1.0)
        eng.memset(selrow[0:1, 1, :, 2 * HD:3 * HD], 1.0).then_inc(self.rows_ready, 1)

    def spread(self, eng):
        for_weights, for_columns = self.banks
        eng.wait_ge(self.transposed, 1)
        eng.tensor_copy(self.wT[:, :, :].rearrange("p n c -> p (n c)"), for_weights[:, :])
        for n in range(2):
            for r in range(3):
                eng.tensor_copy(self.wS[:, n, :, :, HD * (r + 1):HD * (r + 2)].rearrange("p g j c -> p (g j) c"),
                                for_weights[:, n * P:n * P + P].rearrange("p (h c) -> p h c", c=HD))
        eng.wait_ge(self.columns_done, 1)
        eng.tensor_copy(self.cols[:, :, :], for_columns[:, 0:16].rearrange("p (n c) -> p n c", n=2)[:, :, 0:G + 1])\
           .then_inc(self.columns_out, 1)
        eng.wait_ge(self.columns_out, 1)
        for n in range(2):
            eng.tensor_scalar(self.cols_s[:, n, :], self.cols[:, n, 0:G], self.cols[:, n, G:G + 1], None, ALU.mult)


def attention_stage(nc, sh, name, causal, own_weights, x_dram, ctx_dram, weights=None):
    wT, wS, cols, cols_s = own_weights.wT, own_weights.wS, own_weights.cols, own_weights.cols_s
    bvB, boB, va, msp = own_weights.bvB, own_weights.boB, sh.va, sh.msp
    cross = ctx_dram is not None
    ctx = ExitStack()
    with ctx:
        def sb(what, shape, dt=F32):
            return ctx.enter_context(nc.sbuf_tensor(f"{name}_{what}", shape, dt))

        def sem(what):
            return sh.stack.enter_context(nc.semaphore(f"{name}_{what}"))

        x_in = sb("x_in", [P, 2, NT, P])
        c_in = sb("c_in", [P, 2, NT, P]) if cross else x_in
        xT = sb("xT", [P, 2, T])
        cT = sb("cT", [P, 2, T]) if cross else xT
        x_res = sb("x_res", [P, 2, NT, P])
        low = sb("low", [P, 2, T])
        qs = sb("qs", [P, 2, G, T], F32R)
        ks = sb("ks", [P, 2, G, T], F32R)
        qm = sb("qm", [P, 2, G, T], F32R)
        probs = sb("probs", [P, 4, 2, 2, T])
        negmax = sb("negmax", [P, 2, NT, H])
        o_sb = sb("o_sb", [P, 2, 2, T])
        rden = sb("rden", [P, 2, NT, 2, 4])
        ctxn = sb("ctxn", [P, NT, P])
        ctxT = sb("ctxT", [P, T])
        y = sb("y", [P, NT, P])
        stats = sb("stats", [P, NT, 6])
        mv = sb("mv", [P, NT, 2])
        lnv = sb("lnv", [P, NT])
        rstd = sb("rstd", [P, NT])

        bank = sh.bank
        S, TB, O, PR, MISC = bank[0:2], bank[2:4], bank[4:6], bank[6], bank[7]

        x_loaded = [sem("x_loaded0"), sem("x_loaded1")]
        c_loaded = [sem("c_loaded0"), sem("c_loaded1")] if cross else x_loaded
        x_copied = sem("x_copied")
        res_ready = sem("res_ready")
        misc_done = sem("misc_done")
        misc_free = sem("misc_free")
        proj_done = sem("proj_done")
        low_ready = sem("low_ready")
        proj_out = sem("proj_out")
        s_done = sem("s_done")
        max_done = sem("max_done")
        mhi_ready = sem("mhi_ready")
        msp_ready = sem("msp_ready")
        st_done = sem("st_done")
        exp_done = sem("exp_done")
        pv_done = sem("pv_done")
        o_out = sem("o_out")
        rden_ready = sem("rden_ready")
        ctx_ready = sem("ctx_ready")
        stats_ready = sem("stats_ready")
        mv_ready = sem("mv_ready")
        ln_ready = sem("ln_ready")
        rstd_ready = sem("rstd_ready")
        x_normed = sem("x_normed")

        PARTS = (0, 1, 2, 4)
        before = AttnMisc.before

        def wait(eng, s, value):
            if not isinstance(value, int) or value > 0:
                eng.wait_ge(s, value)

        def misc_begin(eng, step, use):
            wait(eng, misc_free, before(step, use))

        def misc_filled(eng, step, use):
            eng.wait_ge(misc_done, before(step, use) + 1)

        def misc_read(eng, step, use):
            eng.wait_ge(misc_free, before(step, use) + 1)

        def steps(eng, body):
            body(-1, 0)
            body(0, 1)
            with eng.Fori(0, (B - 2) // 2) as i:
                body(i * 2 + 1, 0)
                body(i * 2 + 2, 1)
            body(B - 1, 0)
            body(B, 1)

        def has_front(step):
            return not isinstance(step, int) or step < B - 1

        def has_mid(step):
            return not isinstance(step, int) or 0 <= step < B

        def has_tail(step):
            return not isinstance(step, int) or step > 0

        block = ctx.enter_context(nc.Block())

        @block.sync
        def _(eng):
            def load(n, ring):
                if not (isinstance(n, int) and n < 2):
                    misc_read(eng, n - 3, "xT")
                    apart(eng, sh)
                    eng.wait_ge(res_ready, n - 1)
                    apart(eng, sh)
                if not cross:
                    eng.dma_start(x_in[:, ring, :, :], x_dram[:, ds(n * NT, NT), :]).then_inc(x_loaded[ring], 16)
                else:
                    eng.dma_start(c_in[:, ring, :, :], ctx_dram[:, ds(n * NT, NT), :]).then_inc(c_loaded[ring], 16)

            load(0, 0)
            load(1, 1)
            load(2, 0)
            load(3, 1)
            if weights:
                weights.load_constants(eng)
                weights.load(eng, 0)
            with eng.Fori(0, (B - 4) // 2) as i:
                load(i * 2 + 4, 0)
                load(i * 2 + 5, 1)

        @block.gpsimd
        def _(eng):
            def batch(n, ring):
                if cross:
                    if not (isinstance(n, int) and n < 2):
                        misc_read(eng, n - 3, "xT")
                    apart(eng, sh)
                    eng.tensor_copy(x_in[:, ring, :, :], sh.x[:, ds(n * NT, NT), :]).then_inc(x_copied, 1)
                    eng.wait_ge(x_copied, n + 1)
                else:
                    half = n // 2 if isinstance(n, int) else (n - ring) // 2
                    eng.wait_ge(x_loaded[ring], half * 16 + 16)
                if not (isinstance(n, int) and n < 2):
                    misc_read(eng, n - 1, "wo")
                for t in range(NT):
                    add = eng.tensor_tensor(x_res[:, ring, t, :], x_in[:, ring, t, :], boB[:, :], ALU.add)
                add.then_inc(res_ready, 1)

            for n in range(4):
                batch(n, n % 2)
            with eng.Fori(0, (B - 4) // 2) as i:
                batch(i * 2 + 4, 0)
                batch(i * 2 + 5, 1)
            if weights:
                eng.wait_ge(weights.const_in, 48)
                weights.prepare(eng, sh, 0)

        @block.tensor
        def _(eng):
            def in_transposes(n, ring):
                misc_begin(eng, n - 1, "xT")
                if cross:
                    eng.wait_ge(x_copied, n + 1)
                half = n // 2 if isinstance(n, int) else (n - ring) // 2
                eng.wait_ge(c_loaded[ring], half * 16 + 16)
                for t in range(NT):
                    tr = eng.transpose(MISC[:, t * P:t * P + P], x_in[:, ring, t, :], sh.ident[:, :])
                if cross:
                    for t in range(NT):
                        tr = eng.transpose(MISC[:, T + t * P:T + t * P + P], c_in[:, ring, t, :], sh.ident[:, :])
                tr.then_inc(misc_done, 1)

            def project(n, ring, k):
                gp, which = k // 2, k % 2
                if k == 0:
                    misc_read(eng, n - 1, "xT")
                wait(eng, proj_out, n * 4 + k)
                src = xT if which == 0 else cT
                for gi in range(2):
                    mm = eng.matmul(PR[:, gi * T:gi * T + T],
                                    wS[:, which, 2 * gp + gi, :, :].rearrange("p j c -> p (j c)"),
                                    src[:, ring, :], start=True, stop=True)
                mm.then_inc(proj_done, 1)


            def scores(n, ring, u):
                gp, jp, t = u // 4, u % 4 // 2, u % 2
                if u % 4 == 0:
                    eng.wait_ge(proj_out, n * 4 + 2 * gp + 2)
                wait(eng, max_done, n * 8 + u)
                for gi in range(2):
                    for jj in range(2):
                        p = 32 * (2 * jp + jj)
                        mm = eng.matmul(S[jj][:, gi * T:gi * T + T],
                                        qs[p:p + 32, ring, 2 * gp + gi, t * P:t * P + P],
                                        ks[p:p + 32, ring, 2 * gp + gi, :], start=True, stop=not causal)
                    if causal:
                        for bank in S:
                            mm = eng.matmul(bank[:, gi * T + t * P:gi * T + t * P + P], sh.ident_b[:, :],
                                            sh.causal[:, :], start=False, stop=True)
                mm.then_inc(s_done, 1)

            def scores_T(n, ring, u):
                gp, jp, t = u // 4, u % 4 // 2, u % 2
                if u % 4 == 0:
                    misc_read(eng, n if u else n - 1, "mT1" if u else "mT0")
                wait(eng, exp_done, n * 8 + u)
                for gi in range(2):
                    for jj in range(2):
                        p = 32 * (2 * jp + jj)
                        mm = eng.matmul(TB[jj][:, gi * T:gi * T + T],
                                        ks[p:p + 32, ring, 2 * gp + gi, t * P:t * P + P],
                                        qm[p:p + 32, ring, 2 * gp + gi, :], start=True, stop=not causal)
                    if causal:
                        for bank in TB:
                            mm = eng.matmul(bank[:, gi * T + t * P:gi * T + t * P + P], sh.ident_b[:, :],
                                            sh.causal_T[:, :], start=False, stop=True)
                mm.then_inc(st_done, 1)

            def values(n, ring, w):
                gp, jp, gi = w // 4, w % 4 // 2, w % 2
                eng.wait_ge(exp_done, n * 8 + 2 * (w // 2) + 2)
                if w == 0:
                    misc_read(eng, n - 1, "v")
                if w % 4 == 0:
                    wait(eng, o_out, n * 2 + gp - 1)
                for t in range(NT):
                    q0 = t * P if causal else 0
                    for jj in range(2):
                        j = 2 * jp + jj
                        mm = eng.matmul(O[gp][32 * j:32 * j + 32, gi * T + q0:gi * T + T],
                                        va[:, ring, t, 4 * (2 * gp + gi) + j, :],
                                        probs[:, (2 * (w // 2) + t) % 4, jj, gi, q0:T],
                                        start=(t == 0), stop=(t == NT - 1))
                mm.then_inc(pv_done, 1)

            def max_transposes(step, n, ring, gp):
                use = f"mT{gp}"
                misc_begin(eng, step, use)
                eng.wait_ge(msp_ready, n * 2 + gp + 1)
                for gi in range(2):
                    for t in range(NT):
                        g = 2 * gp + gi
                        tr = eng.transpose(MISC[:, gi * T + t * P:gi * T + t * P + P],
                                           msp[:, ring, t, 4 * g:4 * g + 4, :].rearrange("p h c -> p (h c)"),
                                           sh.ident[:, :])
                tr.then_inc(misc_done, 1)

            def out_transposes(step, n, gp):
                misc_begin(eng, step, f"oT{gp}")
                eng.wait_ge(o_out, n * 2 + gp + 1)
                for t in range(NT):
                    for gi in range(2):
                        tr = eng.transpose(MISC[:, (t * 2 + gi) * P:(t * 2 + gi) * P + P],
                                           o_sb[:, gp, gi, t * P:t * P + P], sh.ident[:, :])
                tr.then_inc(misc_done, 1)

            def step(b, other):
                own = 1 - other
                for slot in range(8):
                    if has_front(b) and slot == 0:
                        in_transposes(b + 1, other)
                    if has_mid(b):
                        scores_T(b, own, slot)
                    if has_tail(b) and slot < 2:
                        values(b - 1, other, slot + 6)
                    if has_mid(b) and slot >= 2:
                        values(b, own, slot - 2)
                    if has_front(b) and slot == 7:
                        max_transposes(b, b + 1, other, 0)
                    if has_mid(b) and slot == 3:
                        max_transposes(b, b, own, 1)
                    if has_mid(b) and slot < 2:
                        scores(b, own, slot + 6)
                    if has_front(b) and slot >= 2:
                        scores(b + 1, other, slot - 2)
                    if has_tail(b):
                        if slot == 2:
                            out_transposes(b, b - 1, 1)
                        if slot == 4:
                            misc_begin(eng, b, "cT")
                            eng.wait_ge(ctx_ready, (b - 1) * 4 + 4)
                            for t in range(NT):
                                tr = eng.transpose(MISC[:, t * P:t * P + P], ctxn[:, t, :], sh.ident[:, :])
                            tr.then_inc(misc_done, 1)
                        if slot == 5:
                            misc_begin(eng, b, "wo")
                            for t in range(NT):
                                mm = eng.matmul(MISC[:, t * P:t * P + P], ctxT[:, t * P:t * P + P],
                                                wT[:, 3, :], start=True, stop=True)
                            mm.then_inc(misc_done, 1)
                    if has_front(b) and slot == 1:
                        misc_begin(eng, b, "v")
                        for t in range(NT):
                            mm = eng.matmul(MISC[:, t * P:t * P + P], cT[:, other, t * P:t * P + P],
                                            wT[:, 2, :], start=True, stop=True)
                        mm.then_inc(misc_done, 1)
                    if has_mid(b) and slot == 6:
                        out_transposes(b, b, 0)
                    if has_front(b) and slot in PARTS:
                        project(b + 1, other, PARTS.index(slot))

            steps(eng, step)

        @block.scalar
        def _(eng):
            eng.preload_act_table_set("natural_log_exp_and_others")

            def exps(n, u):
                wait(eng, pv_done, n * 8 + 2 * (u // 2) - 2)
                eng.wait_ge(st_done, n * 8 + u + 1)
                q0 = (u % 2) * P if causal else 0
                eng.activation(probs[:, u % 4, :, :, q0:T],
                               sh.banks[1][:, :].rearrange("p (b a q) -> p b a q", b=2, a=2)[:, :, :, q0:T],
                               ACT.Exp, scale=SM_SCALE).then_inc(exp_done, 1)

            def evac_out(n, gp):
                eng.wait_ge(pv_done, n * 8 + 4 * gp + 4)
                eng.activation(o_sb[:, gp, :, :].rearrange("p g q -> p (g q)"), O[gp][:, :],
                               ACT.Copy).then_inc(o_out, 1)

            def step(b, other):
                for slot in range(8):
                    if has_front(b) and slot == 0:
                        misc_filled(eng, b, "xT")
                        if cross:
                            eng.activation(cT[:, other, :], MISC[:, T:2 * T], ACT.Copy)
                        eng.activation(xT[:, other, :], MISC[:, 0:T], ACT.Copy).then_inc(misc_free, 1)
                    if has_mid(b):
                        exps(b, slot)
                    if has_front(b) and slot in PARTS:
                        k = PARTS.index(slot)
                        gp, which = k // 2, k % 2
                        eng.wait_ge(proj_done, (b + 1) * 4 + k + 1)
                        for gi in range(2):
                            g = 2 * gp + gi
                            hi = eng.activation(low[:, gi, :].bitcast(F32R), PR[:, gi * T:gi * T + T],
                                                ACT.Identity, bias=cols_s[:, which, g:g + 1],
                                                scale=cols[:, which, G:G + 1])
                        hi.then_inc(low_ready, 1)
                    if has_tail(b) and slot == 1:
                        evac_out(b - 1, 1)
                    if has_mid(b) and slot == 5:
                        evac_out(b, 0)
                    if has_tail(b):
                        if slot == 4:
                            misc_filled(eng, b, "cT")
                            eng.activation(ctxT[:, :], MISC[:, 0:T], ACT.Copy).then_inc(misc_free, 1)
                        if slot == 6:
                            eng.wait_ge(mv_ready, b)
                            eng.activation(lnv[:, :], mv[:, :, 1], ACT.Ln, bias=sh.eps[:, 0:1]).then_inc(ln_ready, 1)
                            eng.wait_ge(ln_ready, b)
                            eng.activation(rstd[:, :], lnv[:, :], ACT.Exp, scale=-0.5).then_inc(rstd_ready, 1)

            steps(eng, step)

        @block.vector
        def _(eng):
            def projected(n, ring, k):
                gp, which = k // 2, k % 2
                dst = qs if which == 0 else ks
                eng.wait_ge(low_ready, n * 4 + k + 1)
                for gi in range(2):
                    g = 2 * gp + gi
                    out = eng.scalar_tensor_tensor(out=dst[:, ring, g, :], in0=PR[:, gi * T:gi * T + T],
                                                   scalar=cols[:, which, g:g + 1], in1=low[:, gi, :],
                                                   op0=ALU.add, op1=ALU.subtract)
                out.then_inc(proj_out, 1)

            def maxima(n, ring, u):
                gp, jp, t = u // 4, u % 4 // 2, u % 2
                nk = (t + 1) * P if causal else T
                eng.wait_ge(s_done, n * 8 + u + 1)
                eng.tensor_reduce(negmax[:, ring, t, 8 * gp:8 * gp + 8]
                                  .rearrange("p (a c b) -> p c b a", c=2, b=2)[:, jp, :, :],
                                  sh.banks[0][:, :].rearrange("p (b a k) -> p b a k", b=2, a=2)[:, :, :, 0:nk],
                                  AX.X, ALU.max, negate=True).then_inc(max_done, 1)

            def spread_maxima(n, ring, gp):
                hs = slice(8 * gp, 8 * gp + 8)
                eng.wait_ge(max_done, n * 8 + 4 * gp + 4)
                eng.tensor_copy(msp[:, ring, :, hs, 0:1].bitcast(F32R),
                                negmax[:, ring, :, hs].rearrange("p t (h a) -> p t h a", a=1))\
                   .then_inc(mhi_ready, 1)
                eng.wait_ge(mhi_ready, n * 2 + gp + 1)
                eng.tensor_tensor(msp[:, ring, :, hs, 1], negmax[:, ring, :, hs], msp[:, ring, :, hs, 0],
                                  ALU.subtract).then_inc(msp_ready, 1)

            def less_maxima(step, ring, gp):
                misc_filled(eng, step, f"mT{gp}")
                eng.tensor_tensor(qm[:, ring, 2 * gp:2 * gp + 2, :].rearrange("p g q -> p (g q)"), MISC[:, :],
                                  qs[:, ring, 2 * gp:2 * gp + 2, :].rearrange("p g q -> p (g q)").bitcast(F32),
                                  ALU.add).then_inc(misc_free, 1)

            def normalize(step, n, gp):
                misc_filled(eng, step, f"oT{gp}")
                o4 = MISC[:, :].rearrange("p (t g j c) -> p t (g j) c", t=NT, g=2, j=4)
                eng.reciprocal(rden[:, gp, :, :, :].rearrange("p t g j -> p t (g j)"), o4[:, :, :, HD])\
                   .then_inc(rden_ready, 1)
                eng.wait_ge(rden_ready, n * 2 + gp + 1)
                for t in range(NT):
                    out = eng.tensor_tensor(
                        ctxn[:, t, gp * 64:gp * 64 + 64].rearrange("p (h c) -> p h c", c=HD),
                        o4[:, t, :, 0:HD],
                        rden[:, gp, t, :, :].rearrange("p g (j a) -> p (g j) a", a=1).broadcast_to([P, 8, HD]),
                        ALU.mult)
                    out.then_inc(ctx_ready, 1)
                eng.wait_ge(ctx_ready, n * 4 + gp * 2 + 2)
                eng.sem_inc(misc_free, 1)

            def step(b, other):
                own = 1 - other
                for slot in range(8):
                    if has_front(b) and slot == 7:
                        less_maxima(b, other, 0)
                    if has_mid(b) and slot == 3:
                        less_maxima(b, own, 1)
                    if has_mid(b) and slot < 2:
                        maxima(b, own, slot + 6)
                        if slot == 1:
                            spread_maxima(b, own, 1)
                    if has_front(b) and slot >= 2:
                        maxima(b + 1, other, slot - 2)
                        if slot == 5:
                            spread_maxima(b + 1, other, 0)
                    if has_tail(b):
                        if slot == 2:
                            normalize(b, b - 1, 1)
                        if slot == 5:
                            misc_filled(eng, b, "wo")
                            eng.wait_ge(res_ready, b)
                            eng.tensor_tensor(y[:, :, :], MISC[:, 0:T].rearrange("p (t c) -> p t c", t=NT),
                                              x_res[:, other, :, :], ALU.add).then_inc(misc_free, 1)
                            misc_read(eng, b, "wo")
                            for t in range(NT):
                                st = eng.bn_stats(stats[:, t, :], y[:, t, :])
                            st.then_inc(stats_ready, 1)
                            eng.wait_ge(stats_ready, b)
                            apart(eng, sh)
                            for t in range(NT):
                                ag = eng.bn_aggr(mv[:, t, :], stats[:, t, :])
                            ag.then_inc(mv_ready, 1)
                        if slot == 7:
                            eng.wait_ge(rstd_ready, b)
                            for t in range(NT):
                                out = eng.tensor_scalar(sh.x[:, ds((b - 1) * NT + t, 1), :]
                                                        .rearrange("p a c -> p (a c)"), y[:, t, :],
                                                        mv[:, t, 0:1], rstd[:, t:t + 1],
                                                        ALU.subtract, ALU.mult)
                            out.then_inc(x_normed, 1)
                    if has_front(b) and slot == 1:
                        misc_filled(eng, b, "v")
                        for t in range(NT):
                            out = eng.tensor_tensor(va[:, other, t, :, 0:HD],
                                                    MISC[:, t * P:t * P + P].rearrange("p (h c) -> p h c", c=HD),
                                                    bvB[:, :].rearrange("p (h c) -> p h c", c=HD), ALU.add)
                        out.then_inc(misc_free, 1)
                    if has_mid(b) and slot == 6:
                        normalize(b, b, 0)
                    if has_front(b) and slot in PARTS:
                        projected(b + 1, other, PARTS.index(slot))

            steps(eng, step)
            eng.wait_ge(x_normed, B)


L = 2
FH = 8
FD = 64
INNER = FH * FD
HID = 341
HIDS = [128, 128, HID - 256]
BAND = 192
NORM2 = 2.0 ** 20
START = 3
MAX_INVERSE = 1e12 / 2.0 ** 10
TINY = 1e-30


class FfnMisc:

    FULL = ["hT", "wo", "xT", "mean", "var"]
    PER_LAYER = 5 * B

    @classmethod
    def before(cls, layer, step, use):
        if isinstance(step, int) and (step <= 0 or step >= B - 1):
            base = {-1: 0, 0: 1, B - 1: 5 * (B - 1) - 3, B: 5 * (B - 1) + 1}[step]
            at = 0 if step <= 0 else cls.FULL.index(use) - 1
            assert at >= 0 and (use == "hT") == (step <= 0)
            return layer * cls.PER_LAYER + (base + at)
        return layer * cls.PER_LAYER + step * 5 + (cls.FULL.index(use) - 3)


class LayerWeights:

    LOADS = 14
    STEPS = 8

    def __init__(self, sb, sem, dram):
        self.dram = dram
        self.rot_raw = sb("rot_raw", [P, 2, 2, T])
        self.band_raw = sb("band_raw", [P, BAND + P])
        self.wqkv = sb("wqkv", [P, 3 * INNER])
        self.wo = sb("wo", [P, 4, P])
        self.scol = sb("scol", [P, 2, 2])
        self.rot = sb("rot", [P, 2, 2, T])
        self.wqkvS = sb("wqkvS", [P, 2, 3 * INNER], F32R)
        self.wrotS = sb("wrotS", [P, 2, 2 * FH, 2, 32], F32R)
        self.const_in = sem("const_in")
        self.wa_in = sem("wa_in")
        self.tables = sem("tables")

    def load_constants(self, eng):
        _, _, _, _, rot_d, band_d, band0_d = self.dram
        eng.dma_start(self.rot_raw[:].rearrange("p a b t -> p (a b t)"), rot_d).then_inc(self.const_in, 16)
        eng.dma_start(self.band_raw[:, 0:BAND], band_d).then_inc(self.const_in, 16)
        eng.dma_start(self.band_raw[:, BAND:BAND + P], band0_d).then_inc(self.const_in, 16)

    def load(self, eng, l):
        wqkv_d, qscale_d, kscale_d, wo_d, _, _, _ = self.dram
        scol, wa_in = self.scol, self.wa_in

        def column(d, a, b):
            return d[ds(l, 1), a:b].rearrange("a n -> n a")

        eng.dma_start(self.wqkv[:, :], wqkv_d[ds(l, 1), :, :].rearrange("a k n -> (a k) n")).then_inc(wa_in, 16)
        eng.dma_start(self.wo[:, :, :], wo_d[ds(l, 1), :, :].rearrange("a (c p) n -> p (a c) n", p=P))\
           .then_inc(wa_in, 16)
        for n, d in enumerate((qscale_d, kscale_d)):
            for half in range(2):
                p = half * FD
                eng.dma_start(scol[p:p + FD, n, 0:1], column(d, 0, FD)).then_inc(wa_in, 16)
                eng.dma_start(scol[p:p + 32, n, 1:2], column(d, 32, FD)).then_inc(wa_in, 16)
                eng.dma_start(scol[p + 32:p + FD, n, 1:2], column(d, 0, 32)).then_inc(wa_in, 16)

    def prepare(self, eng, sh, l):
        wqkv, wqkvS, tables = self.wqkv, self.wqkvS, self.tables
        eng.wait_ge(self.wa_in, (l + 1) * (16 * self.LOADS))
        apart(eng, sh)
        eng.tensor_scalar(wqkvS[:, 0, :], wqkv[:, :], 1.0, None, ALU.mult).then_inc(tables, 1)
        eng.wait_ge(tables, l * self.STEPS + 1)
        eng.tensor_tensor(wqkvS[:, 1, :], wqkv[:, :], wqkvS[:, 0, :].bitcast(F32), ALU.subtract)\
           .then_inc(tables, 1)
        eng.wait_ge(tables, l * self.STEPS + 2)
        apart(eng, sh)
        wq = wqkvS[:, :, 0:2 * INNER].rearrange("p e (g s d) -> p e g s d", s=2, d=32)
        for s in range(2):
            eng.tensor_scalar(self.wrotS[:, :, :, s, :], wq[:, :, :, 1 - s, :], 1.0, None,
                              ALU.mult).then_inc(tables, 1)
        for n in range(2):
            for s in range(2):
                eng.tensor_scalar(self.rot[:, n, s, :], self.rot_raw[:, n, s, :], self.scol[:, n, s:s + 1], None,
                                  ALU.mult).then_inc(tables, 1)


def ffn_stage(nc, sh, weights, dram):
    lng_d, lnb_d, w1_d, b1_d, w2_d, b2_d = dram
    wo, rot, wqkvS, wrotS, band_raw = weights.wo, weights.rot, weights.wqkvS, weights.wrotS, weights.band_raw
    const_in, wa_in, tables = weights.const_in, weights.wa_in, weights.tables
    ctx = ExitStack()
    with ctx:
        def sb(what, shape, dt=F32):
            return ctx.enter_context(nc.sbuf_tensor(f"ffn_{what}", shape, dt))

        def sem(what):
            return sh.stack.enter_context(nc.semaphore(f"ffn_{what}"))

        band = sb("band", [P, BAND], BF16)
        band0 = sb("band0", [P, P], BF16)
        ones_head = sb("ones_head", [P, P])
        ones_mean = sb("ones_mean", [P, P])
        tiny = sb("tiny", [P, 1])

        w1S = sb("w1S", [P, 2, 2 * HID], F32R)
        hT = sb("hT", [P, 2, 2, T], F32R)
        hn_now = sb("hn_now", [P, T])
        hn = sb("hn", [P, 2, B * T], F32R)
        PARTS = ((0, 0), (0, 1), (1, 0))
        w1 = sb("w1", [P, 2 * HID])
        w2 = sb("w2", [P, 3, P])
        b1 = sb("b1", [P, 6])
        b2B = sb("b2B", [P, P])
        lgb = sb("lgb", [P, 2])

        x_in = sb("x_in", [P, 2, NT, P])
        squares = sb("squares", [P, 2, 2, T])
        turned = sb("turned", [P, 2, 2, T])
        sums = sb("sums", [P, 4, 2, T])
        capped = sb("capped", [P, 2 * T])
        logs = sb("logs", [P, 2 * T])
        inv = sb("inv", [P, 2, 2 * T])
        qk = sb("qk", [P, 2, 4, 2, T])
        v = sb("v", [P, 2, NT, INNER])
        UNIT_KEYS = [P, BAND]
        negmax = sb("negmax", [P, 2, FH, 2])
        den = sb("den", [P, 2, FH, 2])
        rden = sb("rden", [P, 2, FH, 2])
        raw = [sb("raw0", [P, 2, P]), sb("raw1", [P, 2, BAND])]
        probs = [sb("probs0", [P, 2, P]), sb("probs1", [P, 2, T])]
        probsT = [sb("probsT0", [P, 2, P]), sb("probsT1", [P, 2, T])]
        oT = sb("oT", [P, 4, T])
        x1 = sb("x1", [P, NT, P])
        h1T = sb("h1T", [P, T])
        cen = sb("cen", [P, T])
        cen2 = sb("cen2", [P, T])
        lnv = sb("lnv", [P, T])
        rstd = sb("rstd", [P, T])
        normed = sb("normed", [P, T])
        gate = sb("gate", [P, 3, 2 * T])
        hid = sb("hid", [P, 2, 3, 2 * T])

        PR, NV, S = (sh.bank[0], sh.bank[6]), sh.bank[1], sh.bank[2:4]
        PT, OT, MISC = sh.bank[4], sh.bank[5], sh.bank[7]

        const_set = sem("const_set")
        pool_set = sem("pool_set")
        kept = sem("kept")
        wf_in = sem("wf_in")
        w1_split = sem("w1_split")
        x_copied = sem("x_copied")
        misc_done = sem("misc_done")
        misc_free = sem("misc_free")
        high_ready = sem("high_ready")
        parts_ready = sem("parts_ready")
        proj_done = sem("proj_done")
        squared = sem("squared")
        turned_ready = sem("turned_ready")
        summed = sem("summed")
        nv_done = sem("nv_done")
        nv_free = sem("nv_free")
        capped_ready = sem("capped_ready")
        log_ready = sem("log_ready")
        inv_ready = sem("inv_ready")
        qk_ready = sem("qk_ready")
        s_done = sem("s_done")
        max_done = sem("max_done")
        exp_done = sem("exp_done")
        rden_ready = sem("rden_ready")
        probs_ready = sem("probs_ready")
        pt_done = sem("pt_done")
        pt_out = sem("pt_out")
        pv_done = sem("pv_done")
        o_out = sem("o_out")
        res_ready = sem("res_ready")
        cen_ready = sem("cen_ready")
        cen2_ready = sem("cen2_ready")
        rstd_ready = sem("rstd_ready")
        normed_ready = sem("normed_ready")
        hn_ready = sem("hn_ready")
        w1_done = sem("w1_done")
        gate_ready = sem("gate_ready")
        hid_ready = sem("hid_ready")
        w2_done = sem("w2_done")
        x_ready = sem("x_ready")

        counts = [high_ready, parts_ready, cen2_ready, cen_ready, capped_ready, exp_done, gate_ready, hid_ready,
                  hn_ready, inv_ready, log_ready, max_done, misc_done, misc_free, normed_ready, nv_done,
                  nv_free, o_out, probs_ready, proj_done, pt_done, pt_out, pv_done, qk_ready, rden_ready,
                  res_ready, rstd_ready, s_done, squared, summed, turned_ready, w1_done, w2_done, x_copied,
                  x_ready]
        with nc.Block() as block:
            @block.gpsimd
            def _(eng):
                for count in counts:
                    eng.sem_inc(count, START)

        before = FfnMisc.before
        A_LOADS, F_LOADS = weights.LOADS, 12
        NV_USES = 6

        def misc_begin(eng, l, step, use):
            eng.wait_ge(misc_free, START + before(l, step, use))

        def misc_filled(eng, l, step, use):
            eng.wait_ge(misc_done, START + before(l, step, use) + 1)

        def misc_read(eng, l, step, use):
            eng.wait_ge(misc_free, START + before(l, step, use) + 1)

        def steps(eng, l, body):
            body(l, -1, 0)
            body(l, 0, 1)
            with eng.Fori(0, (B - 2) // 2) as i:
                body(l, i * 2 + 1, 0)
                body(l, i * 2 + 2, 1)
            body(l, B - 1, 0)
            body(l, B, 1)

        def has_front(step):
            return not isinstance(step, int) or step < B - 1

        def has_mid(step):
            return not isinstance(step, int) or 0 <= step < B

        def has_tail(step):
            return not isinstance(step, int) or step > 0

        NORMS = {3: (0, 1), 5: (1, 3), 7: (2, 4)}

        block = ctx.enter_context(nc.Block())

        @block.sync
        def _(eng):
            def load_hidden(l):
                def row(d):
                    return d[ds(l, 1), :].rearrange("a n -> (a n)")

                def column(d, a, b):
                    return d[ds(l, 1), a:b].rearrange("a n -> n a")

                eng.dma_start(lgb[:, 0:1], column(lng_d, 0, P)).then_inc(wf_in, 16)
                eng.dma_start(lgb[:, 1:2], column(lnb_d, 0, P)).then_inc(wf_in, 16)
                eng.dma_start(b2B[:, :], row(b2_d).partition_broadcast(P)).then_inc(wf_in, 16)
                eng.dma_start(w1[:, :], w1_d[ds(l, 1), :, :].rearrange("a k n -> (a k) n")).then_inc(wf_in, 16)
                for n in range(2):
                    for j in range(3):
                        at = n * HID + j * P
                        eng.dma_start(b1[0:HIDS[j], n * 3 + j:n * 3 + j + 1],
                                      column(b1_d, at, at + HIDS[j])).then_inc(wf_in, 16)
                w2l = w2_d[ds(l, 1), :, :].rearrange("a k n -> (a k) n")
                eng.dma_start(w2[:, 0:2, :], w2l[0:256, :].rearrange("(c p) n -> p c n", p=P)).then_inc(wf_in, 16)
                eng.dma_start(w2[0:HIDS[2], 2, :], w2l[256:HID, :]).then_inc(wf_in, 16)

            load_hidden(0)
            with eng.Fori(1, L) as l:
                eng.wait_ge(hn_ready, START + l * B)
                apart(eng, sh)
                weights.load(eng, l)
                eng.wait_ge(x_ready, START + l * (B // 2))
                apart(eng, sh)
                load_hidden(l)

        @block.gpsimd
        def _(eng):
            clears = [(probs[1][:, :, 0:T - BAND], 0.0), (ones_mean[:], 1.0 / P), (tiny[:], TINY),
                      (ones_head[:], 0.0), (ones_head[0:64, 0:64], 1.0), (ones_head[64:128, 64:128], 1.0),
                      (hT[64:128, :, :, 0:1].bitcast(F32), 0.0), (h1T[64:128, 0:1], 0.0)]
            for n, (where, value) in enumerate(clears):
                eng.wait_ge(pool_set, n)
                eng.memset(where, value).then_inc(pool_set, 1)
            eng.wait_ge(pool_set, len(clears))
            eng.tensor_scalar(sh.x0[:, :, :], sh.x[:, 0:B * NT, :], 1.0, None, ALU.mult).then_inc(kept, 1)
            eng.wait_ge(kept, 1)

            def layer(l):
                def add(n, c):
                    eng.wait_ge(turned_ready, START + (l * B + n) * 8 + c + 1)
                    eng.tensor_tensor(sums[:, c // 2, c % 2, :], turned[:, c % 2, 0, :], turned[:, c % 2, 1, :],
                                      ALU.add).then_inc(summed, 1)

                def scale(n, ring, i):
                    eng.wait_ge(inv_ready, START + (l * B + n) * 4 + i + 1)
                    eng.wait_ge(summed, START + (l * B + n) * 8 + 2 * i + 2)
                    eng.wait_ge(qk_ready, START + (l * B + n) * 4 + i)
                    apart(eng, sh)
                    eng.tensor_scalar(capped[:, :], inv[:, i % 2, :], MAX_INVERSE, None, ALU.min)\
                       .then_inc(capped_ready, 1)
                    eng.wait_ge(capped_ready, START + (l * B + n) * 4 + i + 1)
                    apart(eng, sh)
                    eng.tensor_tensor(qk[:, ring, i, :, :].rearrange("p a t -> p (a t)"),
                                      sums[:, i, :, :].rearrange("p a t -> p (a t)"), capped[:, :],
                                      ALU.mult).then_inc(qk_ready, 1)

                def step(l, b, other):
                    own = 1 - other
                    for slot in range(8):
                        if has_mid(b) and slot == 0:
                            scale(b, own, 2)
                            add(b, 7)
                        if has_front(b) and slot >= 1:
                            add(b + 1, slot - 1)
                        if has_mid(b) and slot == 2:
                            scale(b, own, 3)
                        if has_front(b) and slot == 4:
                            scale(b + 1, other, 0)
                        if has_front(b) and slot == 6:
                            scale(b + 1, other, 1)
                        if isinstance(b, int) and b == 0 and slot == 7:
                            eng.wait_ge(wf_in, (l + 1) * (16 * F_LOADS))
                            apart(eng, sh)
                            eng.tensor_scalar(w1S[:, 0, :], w1[:, :], 1.0, None, ALU.mult).then_inc(w1_split, 1)
                            eng.wait_ge(w1_split, l * 2 + 1)
                            eng.tensor_tensor(w1S[:, 1, :], w1[:, :], w1S[:, 0, :].bitcast(F32), ALU.subtract)\
                               .then_inc(w1_split, 1)
                        if has_tail(b) and slot == 5:
                            misc_read(eng, l, b, "wo")
                            for t in range(NT):
                                out = eng.tensor_tensor(sh.x[:, ds((b - 1) * NT + t, 1), :]
                                                        .rearrange("p a c -> p (a c)"), x1[:, t, :], b2B[:, :],
                                                        ALU.add)
                            out.then_inc(res_ready, 1)
                        if has_tail(b) and slot == 7:
                            split_normed(b - 1)

                def split_normed(n):
                    eng.wait_ge(hn_ready, START + l * B + n + 1)
                    apart(eng, sh)
                    at = ds(n * T, T)
                    eng.tensor_copy(hn[:, 0, at], hn_now[:, :]).then_inc(parts_ready, 1)
                    eng.wait_ge(parts_ready, START + (l * B + n) * 2 + 1)
                    apart(eng, sh)
                    eng.tensor_tensor(hn[:, 1, at], hn_now[:, :], hn[:, 0, at].bitcast(F32), ALU.subtract)\
                       .then_inc(parts_ready, 1)

                steps(eng, l, step)

            with eng.Fori(0, L - 1) as l:
                layer(l)
                weights.prepare(eng, sh, l + 1)
            layer(L - 1)

        @block.tensor
        def _(eng):
            eng.wait_ge(pool_set, 8)
            eng.wait_ge(const_set, 1)
            with eng.Fori(0, L) as l:
                eng.wait_ge(wa_in, (l + 1) * (16 * A_LOADS))
                eng.wait_ge(tables, (l + 1) * weights.STEPS)

                def project(n, ring, c):
                    i, which = c // 2, c % 2
                    if c == 0:
                        misc_read(eng, l, n - 1, "hT")
                    eng.wait_ge(turned_ready, START + (l * B + n) * 8 + max(c - 1, 0))
                    at = which * INNER + i * P
                    for nth, (e, f) in enumerate(PARTS):
                        eng.matmul(PR[c % 2][:, 0:T], wqkvS[:, e, at:at + P], hT[:, ring, f, :],
                                   start=(nth == 0), stop=(nth == 2))
                    for nth, (e, f) in enumerate(PARTS):
                        mm = eng.matmul(PR[c % 2][:, T:2 * T],
                                        wrotS[:, e, at // FD:at // FD + 2, :, :].rearrange("p g s d -> p (g s d)"),
                                        hT[:, ring, f, :], start=(nth == 0), stop=(nth == 2))
                    mm.then_inc(proj_done, 1)

                def norms(n, i, nth):
                    eng.wait_ge(squared, START + (l * B + n) * 8 + 2 * i + 2)
                    eng.wait_ge(nv_free, START + (l * B + n) * NV_USES + nth)
                    eng.matmul(NV[:, :], ones_head[:, :], squares[:, i % 2, :, :].rearrange("p a t -> p (a t)"),
                               start=True, stop=True).then_inc(nv_done, 1)

                def values_in(n, ring, t, nth):
                    eng.wait_ge(nv_free, START + (l * B + n) * NV_USES + nth)
                    for i, (e, f) in enumerate(PARTS):
                        mm = eng.matmul(NV[:, :], hT[:, ring, f, t * P:t * P + P], wqkvS[:, e, 2 * INNER:3 * INNER],
                                        start=(i == 0), stop=(i == 2))
                    mm.then_inc(nv_done, 1)

                def scores(n, ring, u):
                    i, t = u // 2, u % 2
                    w = UNIT_KEYS[t]
                    if t == 0:
                        eng.wait_ge(qk_ready, START + (l * B + n) * 4 + i + 1)
                    eng.wait_ge(exp_done, START + (l * B + n) * 8 + u)
                    for hb in range(2):
                        p = 64 * hb
                        eng.matmul(S[hb][:, 0:w], qk[p:p + 64, ring, i, 0, t * P:t * P + P],
                                   qk[p:p + 64, ring, i, 1, (t + 1) * P - w:(t + 1) * P], start=True, stop=False)
                    for hb in range(2):
                        mm = eng.matmul(S[hb][:, 0:w], sh.ident_b[:, :], (band0, band)[t][:, :], start=False,
                                        stop=True)
                    mm.then_inc(s_done, 1)

                def prob_transposes(n, u):
                    t = u % 2
                    eng.wait_ge(probs_ready, START + (l * B + n) * 8 + u + 1)
                    eng.wait_ge(pt_out, START + (l * B + n) * 8 + u)
                    for k in range(2 * (t + 1)):
                        tr = eng.transpose(PT[:, k * P:k * P + P],
                                           probs[t][:, :, :].rearrange("p h k -> p (h k)")[:, k * P:k * P + P],
                                           sh.ident[:, :])
                    tr.then_inc(pt_done, 1)

                def values(n, ring, u):
                    i, t = u // 2, u % 2
                    eng.wait_ge(pt_out, START + (l * B + n) * 8 + u + 1)
                    if u % 4 == 0:
                        eng.wait_ge(o_out, START + (l * B + n) * 2 + u // 4)
                    for k in range(t + 1):
                        for hb in range(2):
                            p, h = 64 * hb, 2 * i + hb
                            mm = eng.matmul(OT[p:p + 64, (i % 2) * T + t * P:(i % 2) * T + t * P + P],
                                            v[:, ring, k, h * FD:h * FD + FD], probsT[t][:, hb, k * P:k * P + P],
                                            start=(k == 0), stop=(k == t))
                    mm.then_inc(pv_done, 1)

                bank_free = [[(turned_ready, B * 8), (nv_free, B * NV_USES)], [(exp_done, B * 8)],
                             [(pt_out, B * 8), (o_out, B * 2)]]

                def up(m, j):
                    if j == 0:
                        eng.wait_ge(parts_ready, START + (l * B + m * 2 + 2) * 2)
                    if isinstance(m, int) and m == 0:
                        eng.wait_ge(wf_in, (l + 1) * (16 * F_LOADS))
                        for free, count in bank_free[j]:
                            eng.wait_ge(free, START + (l + 1) * count)
                    eng.wait_ge(hid_ready, START + (l * 4 + m) * 3 + (j - 2))
                    for n in range(2):
                        at = n * HID + j * P
                        for i, (e, f) in enumerate(PARTS):
                            mm = eng.matmul(sh.bank[2 * j + n][0:HIDS[j], :], w1S[:, e, at:at + HIDS[j]],
                                            hn[:, f, ds(m * (2 * T), 2 * T)], start=(i == 0), stop=(i == 2))
                    mm.then_inc(w1_done, 1)

                def down(m, place):
                    eng.wait_ge(hid_ready, START + (l * 4 + m) * 3 + 3)
                    eng.wait_ge(x_ready, START + l * 4 + m - 1)
                    if place == 1:
                        misc_read(eng, l, B, "var")
                    for t in range(4):
                        for j in range(3):
                            mm = eng.matmul(sh.bank[6 + place][:, t * P:t * P + P],
                                            hid[0:HIDS[j], place, j, t * P:t * P + P], w2[0:HIDS[j], j, :],
                                            start=(j == 0), stop=(j == 2))
                    mm.then_inc(w2_done, 1)

                def step(l, b, other):
                    own = 1 - other
                    for slot in range(8):
                        if has_mid(b):
                            scores(b, own, slot)
                            if slot == 0:
                                project(b, own, 7)
                            if slot == 1:
                                norms(b, 3, 5)
                        if has_front(b):
                            if slot >= 1:
                                project(b + 1, other, slot - 1)
                        if has_tail(b):
                            if slot == 2:
                                misc_begin(eng, l, b, "wo")
                                eng.wait_ge(o_out, START + (l * B + b) * 2)
                                for t in range(NT):
                                    for c in range(4):
                                        mm = eng.matmul(MISC[:, t * P:t * P + P], oT[:, c, t * P:t * P + P],
                                                        wo[:, c, :], start=(c == 0), stop=(c == 3))
                                mm.then_inc(misc_done, 1)
                            if slot == 3:
                                misc_begin(eng, l, b, "xT")
                                for t in range(NT):
                                    tr = eng.transpose(MISC[:, t * P:t * P + P], x1[:, t, :], sh.ident[:, :])
                                tr.then_inc(misc_done, 1)
                            if slot == 4:
                                misc_begin(eng, l, b, "mean")
                                eng.matmul(MISC[:, 0:T], ones_mean[:, :], h1T[:, :], start=True, stop=True)\
                                   .then_inc(misc_done, 1)
                            if isinstance(b, int) and b == B and 2 <= slot <= 4:
                                up(0, slot - 2)
                            if slot == 6:
                                misc_begin(eng, l, b, "var")
                                eng.wait_ge(cen2_ready, START + l * B + b)
                                eng.matmul(MISC[:, 0:T], ones_mean[:, :], cen2[:, :], start=True, stop=True)\
                                   .then_inc(misc_done, 1)
                        if has_front(b):
                            if slot == 2:
                                values_in(b + 1, other, 0, 0)
                            if slot == 3:
                                norms(b + 1, 0, 1)
                            if slot == 4:
                                values_in(b + 1, other, 1, 2)
                            if slot == 5:
                                norms(b + 1, 1, 3)
                            if slot == 7:
                                norms(b + 1, 2, 4)
                        if has_mid(b) and slot >= 1:
                            prob_transposes(b, slot - 1)
                            if slot >= 2:
                                values(b, own, slot - 2)
                        if has_tail(b):
                            if slot == 0:
                                prob_transposes(b - 1, 7)
                                values(b - 1, other, 6)
                            if slot == 1:
                                values(b - 1, other, 7)
                        if has_front(b) and slot == 0:
                            misc_begin(eng, l, b, "hT")
                            eng.wait_ge(x_copied, START + l * B + b + 2)
                            for t in range(NT):
                                tr = eng.transpose(MISC[:, t * P:t * P + P], x_in[:, other, t, :], sh.ident[:, :])
                            tr.then_inc(misc_done, 1)

                steps(eng, l, step)

                with eng.Fori(0, (B // 2 - 2) // 2) as i:
                    for place in (1, 0):
                        m = i * 2 + 2 - place
                        for j in range(3):
                            up(m, j)
                        down(m - 1, 1 - place)
                for j in range(3):
                    up(3, j)
                down(2, 0)
                down(3, 1)

        @block.scalar
        def _(eng):
            eng.wait_ge(pool_set, 8)
            with eng.Fori(0, L) as l:
                eng.preload_act_table_set("natural_log_exp_and_others")

                def shifted(dst, out_sem):
                    eng.activation(dst[0:64, 0:T], MISC[0:64, 0:T], ACT.Copy)
                    eng.activation(dst[64:128, 1:T], MISC[64:128, 0:T - 1], ACT.Copy).then_inc(out_sem, 1)

                def inverses(n, i, nth):
                    N = l * B + n
                    eng.wait_ge(nv_done, START + N * NV_USES + nth + 1)
                    eng.wait_ge(inv_ready, START + N * 4 + i)
                    eng.activation(logs[:, :], NV[:, :], ACT.Ln, scale=NORM2, bias=tiny[:, 0:1]).then_inc(log_ready, 1)
                    eng.wait_ge(log_ready, START + N * 4 + i + 1)
                    eng.sem_inc(nv_free, 1)
                    eng.wait_ge(qk_ready, START + N * 4 + max(i - 1, 0))
                    eng.activation(inv[:, i % 2, :], logs[:, :], ACT.Exp, scale=-0.5).then_inc(inv_ready, 1)

                def exps(n, ring, u):
                    eng.wait_ge(max_done, START + (l * B + n) * 8 + u + 1)
                    eng.wait_ge(probs_ready, START + (l * B + n) * 8 + max(u - 1, 0))
                    for hb in range(2):
                        ex = eng.activation(raw[u % 2][:, hb, :], S[hb][:, 0:UNIT_KEYS[u % 2]], ACT.Exp,
                                            bias=negmax[:, ring, u, hb:hb + 1],
                                            accum_out=den[:, ring, u, hb:hb + 1])
                    ex.then_inc(exp_done, 1)

                def evac_out(n, half):
                    eng.wait_ge(pv_done, START + (l * B + n) * 8 + 4 * half + 4)
                    eng.activation(oT[:, 2 * half:2 * half + 2, :].rearrange("p c t -> p (c t)"), OT[:, :],
                                   ACT.Copy).then_inc(o_out, 1)

                def square(n, c):
                    eng.wait_ge(proj_done, START + (l * B + n) * 8 + c + 1)
                    eng.activation(squares[:, (c // 2) % 2, c % 2, :], PR[c % 2][:, 0:T],
                                   ACT.Square).then_inc(squared, 1)

                def step(l, b, other):
                    own = 1 - other
                    for slot in range(8):
                        if has_mid(b):
                            exps(b, own, slot)
                            if slot == 0:
                                square(b, 7)
                            if slot == 1:
                                inverses(b, 3, 5)
                        if has_front(b):
                            if slot == 0:
                                misc_filled(eng, l, b, "hT")
                                shifted(hT[:, other, 0, :], high_ready)
                            if slot >= 1:
                                square(b + 1, slot - 1)
                            if slot in (2, 4):
                                t = slot // 2 - 1
                                eng.wait_ge(nv_done, START + (l * B + b + 1) * NV_USES + 2 * t + 1)
                                eng.activation(v[:, other, t, :], NV[:, :], ACT.Copy).then_inc(nv_free, 1)
                            if slot in NORMS:
                                inverses(b + 1, *NORMS[slot])
                        if has_tail(b):
                            if slot == 3:
                                misc_filled(eng, l, b, "xT")
                                shifted(h1T, misc_free)
                            if slot == 4:
                                eng.wait_ge(cen_ready, START + l * B + b)
                                eng.activation(cen2[:, :], cen[:, :], ACT.Square).then_inc(cen2_ready, 1)
                            if slot == 6:
                                misc_filled(eng, l, b, "var")
                                eng.activation(lnv[:, :], MISC[:, 0:T], ACT.Ln, bias=sh.eps[:, 0:1])\
                                   .then_inc(misc_free, 1)
                                misc_read(eng, l, b, "var")
                                eng.activation(rstd[:, :], lnv[:, :], ACT.Exp, scale=-0.5).then_inc(rstd_ready, 1)
                            if slot == 1:
                                evac_out(b - 1, 1)
                        if has_mid(b) and slot == 5:
                            evac_out(b, 0)

                steps(eng, l, step)
                eng.preload_act_table_set("gelu_and_others")
                eng.wait_ge(wf_in, (l + 1) * (16 * F_LOADS))
                with eng.Fori(0, 4) as m:
                    for j in range(3):
                        eng.wait_ge(w1_done, START + (l * 4 + m) * 3 + j + 1)
                        eng.wait_ge(hid_ready, START + (l * 4 + m) * 3 + (j - 2))
                        eng.activation(gate[0:HIDS[j], j, :], sh.bank[2 * j + 1][0:HIDS[j], :], ACT.Gelu,
                                       bias=b1[0:HIDS[j], 3 + j:4 + j]).then_inc(gate_ready, 1)

        @block.vector
        def _(eng):
            eng.wait_ge(const_in, 48)
            eng.tensor_copy(band[:, :], band_raw[:, 0:BAND])
            eng.tensor_copy(band0[:, :], band_raw[:, BAND:BAND + P]).then_inc(const_set, 1)
            eng.wait_ge(pool_set, 8)
            with eng.Fori(0, L) as l:
                eng.wait_ge(tables, (l + 1) * weights.STEPS)

                def turn(n, c):
                    i, which = c // 2, c % 2
                    N = l * B + n
                    eng.wait_ge(squared, START + N * 8 + c + 1)
                    eng.wait_ge(summed, START + N * 8 + max(c - 1, 0))
                    eng.tensor_tensor(turned[:, c % 2, :, :].rearrange("p a t -> p (a t)"), PR[c % 2][:, :],
                                      rot[:, which, :, :].rearrange("p a t -> p (a t)"),
                                      ALU.mult).then_inc(turned_ready, 1)

                def maxima(n, ring, u):
                    eng.wait_ge(s_done, START + (l * B + n) * 8 + u + 1)
                    eng.tensor_reduce(negmax[:, ring, u, :],
                                      sh.banks[1][:, :].rearrange("p (h k) -> p h k", h=2)[:, :, 0:UNIT_KEYS[u % 2]],
                                      AX.X, ALU.max, negate=True).then_inc(max_done, 1)

                def normalize(n, ring, u):
                    N = l * B + n
                    eng.wait_ge(exp_done, START + N * 8 + u + 1)
                    eng.reciprocal(rden[:, ring, u, :], den[:, ring, u, :]).then_inc(rden_ready, 1)
                    eng.wait_ge(rden_ready, START + N * 8 + u + 1)
                    eng.wait_ge(pt_done, START + N * 8 + max(u - 1, 0))
                    at = (0, T - BAND)[u % 2]
                    for hb in range(2):
                        out = eng.tensor_scalar(probs[u % 2][:, hb, at:at + UNIT_KEYS[u % 2]], raw[u % 2][:, hb, :],
                                                rden[:, ring, u, hb:hb + 1], None, ALU.mult)
                    out.then_inc(probs_ready, 1)

                def evac_T(n, u):
                    eng.wait_ge(pt_done, START + (l * B + n) * 8 + u + 1)
                    eng.tensor_copy(probsT[u % 2][:, :, :].rearrange("p h k -> p (h k)"),
                                    PT[:, 0:2 * P * (u % 2 + 1)]).then_inc(pt_out, 1)

                def copy_in(n, ring):
                    if not (isinstance(n, int) and n < 2):
                        eng.wait_ge(proj_done, START + (l * B + n - 2) * 8 + 1)
                    eng.tensor_scalar(x_in[:, ring, :, :], sh.x[:, ds(n * NT, NT), :], 1.0, None, ALU.mult)\
                       .then_inc(x_copied, 1)

                def step(l, b, other):
                    own = 1 - other
                    for slot in range(8):
                        if has_tail(b) and slot == 0:
                            evac_T(b - 1, 6)
                        if has_tail(b) and slot == 0:
                            normalize(b - 1, other, 7)
                        if has_front(b) and slot == 0:
                            copy_in(b + 1, other)
                        if has_mid(b) and slot >= 1:
                            normalize(b, own, slot - 1)
                        if has_mid(b):
                            maxima(b, own, slot)
                        if has_tail(b) and slot == 1:
                            evac_T(b - 1, 7)
                        if has_mid(b) and slot >= 2:
                            evac_T(b, slot - 2)
                        if has_mid(b):
                            if slot == 0:
                                turn(b, 7)
                        if has_front(b):
                            if slot == 0:
                                eng.wait_ge(high_ready, START + l * B + b + 2)
                                for p, d in ((0, 0), (64, 1)):
                                    low = eng.tensor_tensor(hT[p:p + 64, other, 1, d:T], MISC[p:p + 64, 0:T - d],
                                                            hT[p:p + 64, other, 0, d:T].bitcast(F32), ALU.subtract)
                                low.then_inc(misc_free, 1)
                            if slot >= 1:
                                turn(b + 1, slot - 1)
                        if has_tail(b):
                            if slot == 2:
                                misc_filled(eng, l, b, "wo")
                                eng.wait_ge(res_ready, START + l * B + b - 1)
                                for t in range(NT):
                                    out = eng.tensor_tensor(x1[:, t, :], MISC[:, t * P:t * P + P],
                                                            sh.x[:, ds((b - 1) * NT + t, 1), :]
                                                            .rearrange("p a c -> p (a c)"), ALU.add)
                                out.then_inc(misc_free, 1)
                            if slot == 4:
                                misc_filled(eng, l, b, "mean")
                                eng.tensor_tensor(cen[:, :], h1T[:, :], MISC[:, 0:T], ALU.subtract)\
                                   .then_inc(cen_ready, 1)
                                eng.wait_ge(cen_ready, START + l * B + b)
                                eng.sem_inc(misc_free, 1)
                            if slot == 7:
                                eng.wait_ge(rstd_ready, START + l * B + b)
                                eng.tensor_tensor(normed[:, :], cen[:, :], rstd[:, :], ALU.mult)\
                                   .then_inc(normed_ready, 1)
                                eng.wait_ge(normed_ready, START + l * B + b)
                                eng.wait_ge(wf_in, (l + 1) * (16 * F_LOADS))
                                eng.wait_ge(parts_ready, START + (l * B + b - 1) * 2)
                                eng.tensor_scalar(hn_now[:, :], normed[:, :], lgb[:, 0:1],
                                                  lgb[:, 1:2], ALU.mult, ALU.add).then_inc(hn_ready, 1)

                steps(eng, l, step)

                def gated(m, place):
                    for j in range(3):
                        eng.wait_ge(gate_ready, START + (l * 4 + m) * 3 + j + 1)
                        eng.scalar_tensor_tensor(out=hid[0:HIDS[j], place, j, :],
                                                 in0=sh.bank[2 * j][0:HIDS[j], :],
                                                 scalar=b1[0:HIDS[j], j:j + 1], in1=gate[0:HIDS[j], j, :],
                                                 op0=ALU.add, op1=ALU.mult).then_inc(hid_ready, 1)

                def add_output(m, place):
                    eng.wait_ge(w2_done, START + l * 4 + m + 1)
                    xs = sh.x[:, ds(m * 4, 4), :].rearrange("p a c -> p (a c)")
                    eng.tensor_tensor(xs, xs, sh.bank[6 + place][:, :], ALU.add).then_inc(x_ready, 1)

                eng.wait_ge(res_ready, START + (l + 1) * B)
                gated(0, 0)
                with eng.Fori(0, (B // 2 - 2) // 2) as i:
                    for place in (1, 0):
                        m = i * 2 + 2 - place
                        gated(m, place)
                        add_output(m - 1, 1 - place)
                gated(3, 1)
                add_output(2, 0)
                add_output(3, 1)
            eng.wait_ge(x_ready, START + L * (B // 2))


def final_stage(nc, sh, out_d):
    ctx = ExitStack()
    with ctx:
        def sb(what, shape, dt=F32):
            return ctx.enter_context(nc.sbuf_tensor(f"last_{what}", shape, dt))

        def sem(what):
            return sh.stack.enter_context(nc.semaphore(f"last_{what}"))

        N = B * NT
        y = sb("y", [P, N, P])
        out = sb("out", [P, N, P])
        stats = sb("stats", [P, N, 6])
        mv = sb("mv", [P, N, 2])
        lnv = sb("lnv", [P, N])
        rstd = sb("rstd", [P, N])
        summed, measured, aggregated, logged, rooted, scaled, stored = (
            sem(w) for w in ("summed", "measured", "aggregated", "logged", "rooted", "scaled", "stored"))
        block = ctx.enter_context(nc.Block())

        @block.vector
        def _(eng):
            for q in range(2):
                a, b = q * N // 2, (q + 1) * N // 2
                eng.tensor_tensor(y[:, a:b, :], sh.x0[:, a:b, :], sh.x[:, a:b, :], ALU.add).then_inc(summed, 1)
            for n in range(N):
                if n % (N // 2) == 0:
                    eng.wait_ge(summed, n // (N // 2) + 1)
                eng.bn_stats(stats[:, n, :], y[:, n, :]).then_inc(measured, 1)
            for n in range(N):
                eng.wait_ge(measured, n + 1)
                eng.bn_aggr(mv[:, n, :], stats[:, n, :]).then_inc(aggregated, 1)
            eng.wait_ge(rooted, 1)
            for n in range(N):
                eng.tensor_scalar(out[:, n, :], y[:, n, :], mv[:, n, 0:1], rstd[:, n:n + 1], ALU.subtract,
                                  ALU.mult).then_inc(scaled, 1)

        @block.scalar
        def _(eng):
            eng.preload_act_table_set("natural_log_exp_and_others")
            eng.wait_ge(aggregated, N)
            eng.activation(lnv[:, :], mv[:, :, 1], ACT.Ln, bias=sh.eps[:, 0:1]).then_inc(logged, 1)
            eng.wait_ge(logged, 1)
            eng.activation(rstd[:, :], lnv[:, :], ACT.Exp, scale=-0.5).then_inc(rooted, 1)

        @block.sync
        def _(eng):
            for q in range(4):
                a, b = q * N // 4, (q + 1) * N // 4
                eng.wait_ge(scaled, b)
                eng.dma_start(out_d[:, a:b, :], out[:, a:b, :]).then_inc(stored, 16)
            eng.wait_ge(stored, 64)


def build(nc, args, out):
    x_d = args["x"].rearrange("b (t p) d -> p (b t) d", p=P)
    ctx_d = args["ctx_1024"].rearrange("b (t p) d -> p (b t) d", p=P)
    out_d = out.rearrange("b (t p) d -> p (b t) d", p=P)
    sh = Shared()
    stack = ExitStack()
    sh.stack = stack
    with stack:
        def sb(name, shape, dt=F32):
            return stack.enter_context(nc.sbuf_tensor(name, shape, dt))

        sh.x = sb("x_all", [P, B * NT, P])
        sh.x0 = sb("x0", [P, B * NT, P])
        sh.ident = sb("ident", [P, P])
        sh.ident_b = sb("ident_b", [P, P], BF16)
        sh.causal = sb("causal", [P, P], BF16)
        sh.causal_T = sb("causal_T", [P, P], BF16)
        sh.one = sb("one", [1, 1])
        sh.eps = sb("eps", [P, 1])
        cm = sb("causal_raw", [P, 2, P])
        sh.banks = [stack.enter_context(nc.psum_tensor(f"banks{i}", [P, 2 * 512], F32)) for i in range(4)]
        sh.bank = [sh.banks[i // 2][:, (i % 2) * 512:(i % 2) * 512 + 512] for i in range(8)]
        const_loaded = stack.enter_context(nc.semaphore("const_loaded"))
        ident_loaded = stack.enter_context(nc.semaphore("ident_loaded"))
        one_ready = stack.enter_context(nc.semaphore("one_ready"))
        sh.passed = stack.enter_context(nc.semaphore("passed"))
        va_cleared = stack.enter_context(nc.semaphore("va_cleared"))
        f = "L0_ffn_"
        weights = LayerWeights(lambda what, shape, dt=F32: sb(f"ffn_{what}", shape, dt),
                               lambda what: stack.enter_context(nc.semaphore(f"ffn_{what}")),
                               [args[f + k] for k in ("wqkv", "q_scale", "k_scale", "wo")]
                               + [args[k] for k in ("c_rot", "c_band", "c_band0")])
        attn_memory = stack.enter_context(ExitStack())

        def attn_sb(name, shape, dt=F32):
            return attn_memory.enter_context(nc.sbuf_tensor(name, shape, dt))

        sh.va = attn_sb("va", [P, 2, NT, H, 32])
        sh.msp = attn_sb("msp", [P, 2, NT, H, 32])
        attn = [AttnWeights(lambda what, shape, dt=F32, name=name: attn_sb(f"{name}_{what}", shape, dt),
                            lambda what, name=name: stack.enter_context(nc.semaphore(f"{name}_{what}")),
                            [args[p + k] for k in ("Wq", "Wk", "Wv", "Wo", "bq", "bk", "bv", "bo")],
                            sh.bank[at:at + 2])
                for name, p, at in (("self", "L0_attn_", 4), ("cross", "L0_xattn_", 6))]
        with nc.Block() as block:
            @block.sync
            def _(eng):
                eng.dma_start(sh.ident[:, :], args["c_ident"]).then_inc(ident_loaded, 16)
                attn[0].load(eng)
                eng.dma_start(cm[:, 0, :], args["c_causal"]).then_inc(const_loaded, 16)
                eng.dma_start(cm[:, 1, :], args["c_causal_T"]).then_inc(const_loaded, 16)
                attn[1].load(eng)

            @block.gpsimd
            def _(eng):
                eng.memset(sh.va[:], 0.0).then_inc(va_cleared, 1)
                eng.wait_ge(va_cleared, 1)
                eng.memset(sh.va[:, :, :, :, HD:HD + 1], 1.0)
                eng.memset(sh.msp[:], 0.0)

            @block.tensor
            def _(eng):
                eng.wait_ge(one_ready, 1)
                eng.wait_ge(ident_loaded, 16)
                for w in attn:
                    w.transpose(eng, sh)

            @block.vector
            def _(eng):
                eng.memset(sh.one[:, :], 1.0).then_inc(one_ready, 1)
                eng.memset(sh.eps[:, :], EPS)
                for w in attn:
                    w.clear(eng)
                attn[0].lay_rows(eng)
                attn[0].spread(eng)
                eng.wait_ge(const_loaded, 32)
                eng.wait_ge(ident_loaded, 16)
                eng.tensor_copy(sh.ident_b[:, :], sh.ident[:, :])
                eng.tensor_copy(sh.causal[:, :], cm[:, 0, :])
                eng.tensor_copy(sh.causal_T[:, :], cm[:, 1, :])
                attn[1].lay_rows(eng)
                attn[1].spread(eng)

        for name, causal, cd in (("self", True, None), ("cross", False, ctx_d)):
            attention_stage(nc, sh, name, causal, attn[cd is not None],
                            x_d, cd, weights if cd is not None else None)

        attn_memory.close()
        ffn_stage(nc, sh, weights, [args[f + k] for k in ("ln_g", "ln_b", "w1", "b1", "w2", "b2")])
        final_stage(nc, sh, out_d)


NEG = -1e30


def host_constants(np):
    i = np.arange(P)
    causal = np.where(i[None, :] <= i[:, None], 0, NEG).astype(np.float32)
    gap = np.arange(BAND)[None, :] - i[:, None]
    band = np.where((gap >= 0) & (gap <= 64), 0, NEG).astype(np.float32)
    gap0 = i[:, None] - i[None, :]
    band0 = np.where((gap0 >= 0) & (gap0 <= 64), 0, NEG).astype(np.float32)
    half = np.arange(0, FD, 2, dtype=np.float32)
    inv_freq = (1.0 / np.power(np.float32(10000.0), half / np.float32(FD))).astype(np.float32)
    t = np.arange(T, dtype=np.float32)
    freqs = np.concatenate([t[:, None] * inv_freq[None, :]] * 2, axis=-1)
    base = ((half + np.float32(0.4 * FD)) / np.float32(1.4 * FD)).astype(np.float32)
    power = (t - T // 2) / np.float32(32.0)
    scale = np.power(base[None, :], power[:, None]).astype(np.float32)
    scale = np.concatenate([scale, scale], axis=-1)
    cos, sin = np.cos(freqs), np.sin(freqs)
    sign = np.where(np.arange(FD) < FD // 2, -1.0, 1.0).astype(np.float32)[None, :]
    root = np.float32(NORM2 ** 0.5)
    rot = np.zeros((2, 2, FD, T), np.float32)
    rot[0, 0] = (cos * scale).T * (8 * root)
    rot[0, 1] = (sign * sin * scale).T * (8 * root)
    rot[1, 0] = (cos / scale).T * root
    rot[1, 1] = (sign * sin / scale).T * root
    rot = np.concatenate([rot, rot], axis=2).transpose(2, 0, 1, 3).reshape(P, 4 * T)
    return {"c_ident": np.eye(P, dtype=np.float32), "c_causal": causal, "c_causal_T": np.ascontiguousarray(causal.T),
            "c_rot": np.ascontiguousarray(rot.astype(np.float32)), "c_band": band, "c_band0": band0}



def kernel(**inputs):
    import numpy as np
    import concourse.bacc as bacc
    from concourse.bass_utils import run_bass_kernel_spmd as run

    nc = bacc.Bacc("TRN2", target_bir_lowering=False, num_devices=1)
    arrays, args = {}, {}
    for name, a in list(inputs.items()) + list(host_constants(np).items()):
        a = np.ascontiguousarray(a)
        arrays[f"in_{name}_dram"] = a
        args[name] = nc.dram_tensor(f"in_{name}_dram", a.shape, mybir.dt.from_np(a.dtype), kind="ExternalInput").ap()
    out = nc.dram_tensor("out_0_dram", (B, T, P), F32, kind="ExternalOutput").ap()
    build(nc, args, out)
    r = run(nc, [arrays], core_ids=[0])
    return r.results[0]["out_0_dram"]
```
